# Optimizing a Trainium2 kernel written in Bass

```python
import numpy as np
import jax
import jax.numpy as jnp

def _softmax(x, axis=-1):
    return jax.nn.softmax(x, axis=axis)

def _gelu(x):
    return jax.nn.gelu(x, approximate=True)

def _silu(x):
    return jax.nn.silu(x)

def _sigmoid(x):
    return jax.nn.sigmoid(x)

def _layernorm(x, axis=-1, eps=1e-05):
    m = jnp.mean(x, axis=axis, keepdims=True)
    v = jnp.var(x, axis=axis, keepdims=True)
    return (x - m) / jnp.sqrt(v + eps)

def _scatter_add(tgt, idx, src, axis=0):
    return tgt.at[idx].add(src)

def _segment_sum(src, seg, n):
    return jax.ops.segment_sum(src, seg, n)
kernel_name = 'mk_seq_postln_d1_jaxref_r8_fe7d10'

def setup_inputs(seed: int=0):
    np.random.seed(seed)
    _w = jnp.asarray

    def _L0_attn_setup():
        import jax, jax.numpy as jnp
        import numpy as np
        from jax import lax
        D_MODEL, D_STATE, D_CONV, EXPAND = (128, 16, 4, 2)
        D_INNER = D_MODEL * EXPAND
        BATCH, SEQ = (4, 256)

        def _mamba_forward(x, W_in, conv_w, conv_b, W_x, W_dt, b_dt, A_log, D, W_out):
            batch, seq_len, _ = x.shape
            xz = x @ W_in
            x_in, z = jnp.split(xz, 2, axis=-1)
            x_c = lax.conv_general_dilated(x_in.transpose(0, 2, 1), conv_w, window_strides=(1,), padding=[(D_CONV - 1, 0)], feature_group_count=D_INNER, dimension_numbers=('NCH', 'OIH', 'NCH')) + conv_b[None, :, None]
            x_conv = jax.nn.silu(x_c.transpose(0, 2, 1))
            A = -jnp.exp(A_log)
            Bm, Cm = jnp.split(x_conv @ W_x, 2, axis=-1)
            dt = jax.nn.softplus(x_conv @ W_dt + b_dt)

            def step(h, ins):
                u_t, dt_t, B_t, C_t = ins
                dA = jnp.exp(dt_t[:, :, None] * A)
                h = dA * h + (dt_t * u_t)[:, :, None] * B_t[:, None, :]
                y_t = jnp.einsum('bdn,bn->bd', h, C_t)
                return (h, y_t)
            h0 = jnp.zeros((batch, D_INNER, D_STATE), dtype=x.dtype)
            xs = (x_conv.transpose(1, 0, 2), dt.transpose(1, 0, 2), Bm.transpose(1, 0, 2), Cm.transpose(1, 0, 2))
            _, ys = lax.scan(step, h0, xs)
            y = ys.transpose(1, 0, 2)
            y = y + x_conv * D
            y = y * jax.nn.silu(z)
            return y @ W_out
        key = jax.random.key(seed)
        ks = jax.random.split(key, 9)
        s = lambda fan_in: 1.0 / np.sqrt(fan_in)
        return {'x': jax.random.normal(ks[0], (BATCH, SEQ, D_MODEL), dtype=jnp.float32), 'W_in': jax.random.normal(ks[1], (D_MODEL, 2 * D_INNER), dtype=jnp.float32) * s(D_MODEL), 'conv_w': jax.random.normal(ks[2], (D_INNER, 1, D_CONV), dtype=jnp.float32) * s(D_CONV), 'conv_b': jax.random.normal(ks[3], (D_INNER,), dtype=jnp.float32) * 0.01, 'W_x': jax.random.normal(ks[4], (D_INNER, 2 * D_STATE), dtype=jnp.float32) * s(D_INNER), 'W_dt': jax.random.normal(ks[5], (D_INNER, D_INNER), dtype=jnp.float32) * s(D_INNER), 'b_dt': jax.random.normal(ks[6], (D_INNER,), dtype=jnp.float32) * 0.01, 'A_log': jnp.log(jnp.arange(1, D_STATE + 1, dtype=jnp.float32)), 'D': jnp.ones((D_INNER,), dtype=jnp.float32), 'W_out': jax.random.normal(ks[7], (D_INNER, D_MODEL), dtype=jnp.float32) * s(D_INNER)}
    _L0_attn_in = _L0_attn_setup()

    def _L0_ffn_setup():
        import jax, jax.numpy as jnp
        import numpy as np
        N_EXP = 8
        TOP_K = 2
        CAP_FACTOR = 1.25
        NEG_INF = -1000000000.0

        def _moe_forward(x, w_g, c_fc, c_proj):
            B, T, D = x.shape
            N = B * T
            xf = x.reshape(N, D)
            logits = xf @ w_g
            topv, topi = jax.lax.top_k(logits, TOP_K)
            full = jnp.full_like(logits, NEG_INF)
            full = full.at[jnp.arange(N)[:, None], topi].set(topv)
            probs = jax.nn.softmax(full, axis=-1)
            capacity = int(TOP_K * CAP_FACTOR * N / N_EXP)
            capacity += capacity % 2
            mask = jax.nn.one_hot(jnp.swapaxes(topi, 0, 1), N_EXP, dtype=jnp.int32)
            rank = jnp.cumsum(mask.reshape(TOP_K * N, N_EXP), axis=0).reshape(TOP_K, N, N_EXP) - 1
            mask = mask * (rank < capacity)
            rank_sel = jnp.sum(mask * rank, axis=-1)
            wts = jnp.sum(mask * probs[None], axis=-1)
            cb = jnp.zeros((N, N_EXP, capacity), x.dtype)
            tok = jnp.arange(N)
            for k in range(TOP_K):
                cb = cb.at[tok, topi[:, k], rank_sel[k]].add(wts[k])
            sec_mask = (cb != 0).astype(x.dtype)
            exp_batches = jnp.einsum('nec,nd->ecd', sec_mask, xf)
            h = jax.nn.gelu(jnp.einsum('ecd,edh->ech', exp_batches, c_fc), approximate=False)
            exp_out = jnp.einsum('ech,ehd->ecd', h, c_proj)
            out = jnp.einsum('nec,ecd->nd', cb, exp_out)
            return out.reshape(B, T, D)
        key = jax.random.key(seed)
        k1, k2, k3, k4 = jax.random.split(key, 4)
        B, T, D = (4, 64, 128)
        H = 4 * D
        x = jax.random.normal(k1, (B, T, D), jnp.float32)
        w_g = jax.random.normal(k2, (D, N_EXP), jnp.float32) * 0.02
        c_fc = jax.random.normal(k3, (N_EXP, D, H), jnp.float32) * 0.02
        c_proj = jax.random.normal(k4, (N_EXP, H, D), jnp.float32) * 0.02
        return {'x': x, 'w_g': w_g, 'c_fc': c_fc, 'c_proj': c_proj}
    _L0_ffn_in = _L0_ffn_setup()
    _d = {'L0_attn_x': _L0_attn_in['x'], 'L0_attn_W_in': _L0_attn_in['W_in'], 'L0_attn_conv_w': _L0_attn_in['conv_w'], 'L0_attn_conv_b': _L0_attn_in['conv_b'], 'L0_attn_W_x': _L0_attn_in['W_x'], 'L0_attn_W_dt': _L0_attn_in['W_dt'], 'L0_attn_b_dt': _L0_attn_in['b_dt'], 'L0_attn_A_log': _L0_attn_in['A_log'], 'L0_attn_D': _L0_attn_in['D'], 'L0_attn_W_out': _L0_attn_in['W_out'], 'L0_ffn_w_g': _L0_ffn_in['w_g'], 'L0_ffn_c_fc': _L0_ffn_in['c_fc'], 'L0_ffn_c_proj': _L0_ffn_in['c_proj']}
    _x0 = _d['L0_attn_x']
    _d['L0_attn_x'] = jax.random.normal(jax.random.fold_in(jax.random.key(seed), 1), (2, 1024, 128), dtype=_x0.dtype)
    del _x0
    return _d

def reference(L0_attn_x, L0_attn_W_in, L0_attn_conv_w, L0_attn_conv_b, L0_attn_W_x, L0_attn_W_dt, L0_attn_b_dt, L0_attn_A_log, L0_attn_D, L0_attn_W_out, L0_ffn_w_g, L0_ffn_c_fc, L0_ffn_c_proj):

    def _L0_attn_ref(x, W_in, conv_w, conv_b, W_x, W_dt, b_dt, A_log, D, W_out):
        import jax, jax.numpy as jnp
        import numpy as np
        from jax import lax
        D_MODEL, D_STATE, D_CONV, EXPAND = (128, 16, 4, 2)
        D_INNER = D_MODEL * EXPAND
        BATCH, SEQ = (4, 256)

        def _mamba_forward(x, W_in, conv_w, conv_b, W_x, W_dt, b_dt, A_log, D, W_out):
            batch, seq_len, _ = x.shape
            xz = x @ W_in
            x_in, z = jnp.split(xz, 2, axis=-1)
            x_c = lax.conv_general_dilated(x_in.transpose(0, 2, 1), conv_w, window_strides=(1,), padding=[(D_CONV - 1, 0)], feature_group_count=D_INNER, dimension_numbers=('NCH', 'OIH', 'NCH')) + conv_b[None, :, None]
            x_conv = jax.nn.silu(x_c.transpose(0, 2, 1))
            A = -jnp.exp(A_log)
            Bm, Cm = jnp.split(x_conv @ W_x, 2, axis=-1)
            dt = jax.nn.softplus(x_conv @ W_dt + b_dt)

            def step(h, ins):
                u_t, dt_t, B_t, C_t = ins
                dA = jnp.exp(dt_t[:, :, None] * A)
                h = dA * h + (dt_t * u_t)[:, :, None] * B_t[:, None, :]
                y_t = jnp.einsum('bdn,bn->bd', h, C_t)
                return (h, y_t)
            h0 = jnp.zeros((batch, D_INNER, D_STATE), dtype=x.dtype)
            xs = (x_conv.transpose(1, 0, 2), dt.transpose(1, 0, 2), Bm.transpose(1, 0, 2), Cm.transpose(1, 0, 2))
            _, ys = lax.scan(step, h0, xs)
            y = ys.transpose(1, 0, 2)
            y = y + x_conv * D
            y = y * jax.nn.silu(z)
            return y @ W_out
        return _mamba_forward(x, W_in, conv_w, conv_b, W_x, W_dt, b_dt, A_log, D, W_out)

    def _L0_ffn_ref(x, w_g, c_fc, c_proj):
        import jax, jax.numpy as jnp
        import numpy as np
        N_EXP = 8
        TOP_K = 2
        CAP_FACTOR = 1.25
        NEG_INF = -1000000000.0

        def _moe_forward(x, w_g, c_fc, c_proj):
            B, T, D = x.shape
            N = B * T
            xf = x.reshape(N, D)
            logits = xf @ w_g
            topv, topi = jax.lax.top_k(logits, TOP_K)
            full = jnp.full_like(logits, NEG_INF)
            full = full.at[jnp.arange(N)[:, None], topi].set(topv)
            probs = jax.nn.softmax(full, axis=-1)
            capacity = int(TOP_K * CAP_FACTOR * N / N_EXP)
            capacity += capacity % 2
            mask = jax.nn.one_hot(jnp.swapaxes(topi, 0, 1), N_EXP, dtype=jnp.int32)
            rank = jnp.cumsum(mask.reshape(TOP_K * N, N_EXP), axis=0).reshape(TOP_K, N, N_EXP) - 1
            mask = mask * (rank < capacity)
            rank_sel = jnp.sum(mask * rank, axis=-1)
            wts = jnp.sum(mask * probs[None], axis=-1)
            cb = jnp.zeros((N, N_EXP, capacity), x.dtype)
            tok = jnp.arange(N)
            for k in range(TOP_K):
                cb = cb.at[tok, topi[:, k], rank_sel[k]].add(wts[k])
            sec_mask = (cb != 0).astype(x.dtype)
            exp_batches = jnp.einsum('nec,nd->ecd', sec_mask, xf)
            h = jax.nn.gelu(jnp.einsum('ecd,edh->ech', exp_batches, c_fc), approximate=False)
            exp_out = jnp.einsum('ech,ehd->ecd', h, c_proj)
            out = jnp.einsum('nec,ecd->nd', cb, exp_out)
            return out.reshape(B, T, D)
        return _moe_forward(x, w_g, c_fc, c_proj)
    x = L0_attn_x
    x = _layernorm(x + _L0_attn_ref(x, L0_attn_W_in, L0_attn_conv_w, L0_attn_conv_b, L0_attn_W_x, L0_attn_W_dt, L0_attn_b_dt, L0_attn_A_log, L0_attn_D, L0_attn_W_out), axis=-1)
    x = _layernorm(x + _L0_ffn_ref(x, L0_ffn_w_g, L0_ffn_c_fc, L0_ffn_c_proj), axis=-1)
    return x

_drawn_inputs = setup_inputs


def setup_inputs(seed=0):
    import zlib

    import numpy as np

    out = dict(_drawn_inputs(seed))
    spreads = {'L0_attn_D': (1.0, 0.2)}
    factors = {'L0_attn_conv_b': 8.0, 'L0_attn_b_dt': 8.0}
    for name, (base, spread) in spreads.items():
        noise = np.random.default_rng([zlib.crc32(name.encode()), seed]).standard_normal(out[name].shape)
        drawn = base * np.exp(spread * noise) if base else spread * noise
        out[name] = jnp.asarray(drawn.astype(out[name].dtype))
    for name, factor in factors.items():
        out[name] = (out[name] * factor).astype(out[name].dtype)
    return out
```

```python
from contextlib import ExitStack

import numpy as np

import concourse.bass as bass
from concourse import mybir
from concourse.alu_op_type import AluOpType as ALU

F32 = mybir.dt.float32
BF16 = mybir.dt.bfloat16
U32 = mybir.dt.uint32
ACT = mybir.ActivationFunctionType
AX = mybir.AxisListType

P = 128
BATCH, SEQ, D_MODEL = 2, 1024, 128
D_INNER, D_STATE, D_CONV = 256, 16, 4
TOKENS = BATCH * SEQ
DT = D_INNER // P
CH = 512
NCH = SEQ // CH
NQ = TOKENS // CH
TILES = TOKENS // P
TPC = CH // P
PAD = D_CONV - 1
N_EXP, TOP_K, D_HID = 8, 2, 512
HT = D_HID // P
NEG_INF = -1000000000.0
CAPACITY = int(TOP_K * 1.25 * TOKENS / N_EXP)
CAPACITY += CAPACITY % 2
SLOT_TILES = CAPACITY // P
assert SLOT_TILES * P == CAPACITY
SLOTS = N_EXP * CAPACITY
PAIRS = N_EXP // 2
HALF = CAPACITY // 2
RUNS = TOP_K * TILES
EPS = 1e-05
UNITS = NCH * DT
BIG = 1e30


class Tally:

    def __init__(self):
        self.n = 0

    def up(self, k=1):
        self.n += k
        return self.n


def layer_program(nc, x, W_in, channel_values, W_x, W_dt, A_log, W_out, w_g, c_fc, c_proj, out):
    with ExitStack() as ctx:
        def sb(name, shape, dt=F32):
            return ctx.enter_context(nc.sbuf_tensor(name, shape, dt))

        def sem(name):
            return ctx.enter_context(nc.semaphore(name))

        slot_rows = nc.dram_tensor("slot_rows", [SLOTS, D_MODEL], F32, kind="Internal").ap()
        expert_rows = nc.dram_tensor("expert_rows", [SLOTS, D_MODEL], F32, kind="Internal").ap()

        w_in_sb = sb("w_in_sb", [P, 2 * D_INNER])
        channel_sb = sb("channel_sb", [P, DT, D_CONV + 3])
        conv_w_sb = channel_sb[:, :, 0:D_CONV]
        conv_b_sb, b_dt_sb, d_sb = (channel_sb[:, :, D_CONV + k] for k in range(3))
        a_log_sb = sb("a_log_sb", [P, D_STATE])
        a_exp = sb("a_exp", [P, D_STATE])
        a_neg = sb("a_neg", [P, UNITS, D_STATE])
        w_x_sb = sb("w_x_sb", [P, DT, 2 * D_STATE])
        w_x4 = sb("w_x4", [P, DT, 4, 2 * D_STATE])
        w_dt_sb = sb("w_dt_sb", [P, DT, D_INNER])
        w_out_sb = sb("w_out_sb", [P, DT, D_MODEL])
        w_g_sb = sb("w_g_sb", [P, N_EXP])
        ident = sb("ident", [P, P])
        diag_d = sb("diag_d", [P, DT, P])
        pick = sb("pick", [P, 2 * D_STATE], BF16)
        selector = sb("selector", [P, 2 * D_STATE, P], BF16)
        upto = sb("upto", [P, P], BF16)
        ones = sb("ones", [P, P], BF16)
        zeros = sb("zeros", [P, SLOTS // P * D_MODEL // 8])

        x_tok = sb("x_tok", [P, TILES, D_MODEL])
        x_chan = sb("x_chan", [P, TOKENS])
        x_in = sb("x_in", [P, DT, BATCH, PAD + SEQ])
        z_gate = sb("z_gate", [P, DT, TOKENS])
        u = sb("u", [P, DT, TOKENS])
        dt = sb("dt", [P, DT, TOKENS])
        dtu = sb("dtu", [P, DT, TOKENS])
        bc_parts = sb("bc_parts", [P, TOKENS], BF16)
        bc_rest = sb("bc_rest", [P, CH])
        soft = sb("soft", [P, 2, CH])

        drive = sb("drive", [P, NCH, DT, CH])
        state = sb("state", [P, NCH, DT, CH])
        product = sb("product", [P, NCH, DT, CH])
        c_wide = sb("c_wide", [P, NCH, CH])
        y_first = sb("y_first", [P, NCH, DT, CH])

        x1 = sb("x1", [P, TILES, D_MODEL])
        stats = sb("stats", [P, TILES, 6])
        moments = sb("moments", [P, TILES, 2])
        log_var = sb("log_var", [P, TILES])
        rstd = sb("rstd", [P, TILES])
        newton = sb("newton", [P, TILES])
        countdown = sb("countdown", [P, N_EXP])
        logits = sb("logits", [P, TILES, N_EXP])
        logits2 = sb("logits2", [P, TILES, N_EXP])
        keys = sb("keys", [P, TILES, N_EXP])
        top = sb("top", [P, TOP_K, TILES])
        top_key = sb("top_key", [P, TOP_K, TILES])
        chosen = sb("chosen", [P, RUNS, N_EXP])
        chosen_bf = sb("chosen_bf", [P, RUNS, N_EXP], BF16)
        peak = sb("peak", [P, TILES])
        above = sb("above", [P, TOP_K + 1, TILES])
        exps = sb("exps", [P, TOP_K + 1, TILES])
        denom = sb("denom", [P, TILES])
        weight = sb("weight", [P, RUNS])
        run_totals = sb("run_totals", [P, N_EXP, RUNS])
        run_keep = sb("run_keep", [P, N_EXP, RUNS])
        run_upto = sb("run_upto", [P, N_EXP, RUNS])
        ranks = sb("ranks", [P, RUNS, N_EXP])
        rank = sb("rank", [P, RUNS])
        kept = sb("kept", [P, RUNS])
        slot = sb("slot", [P, RUNS])
        slot_out = sb("slot_out", [P, RUNS])
        slot_in = sb("slot_in", [P, RUNS])
        scatter_at = sb("scatter_at", [P, RUNS], U32)
        gather_at = sb("gather_at", [P, RUNS], U32)

        fc_sb = sb("fc_sb", [P, 2, D_HID])
        proj_sb = sb("proj_sb", [P, 2, HT, D_MODEL])
        rows_in = sb("rows_in", [P, 2, SLOT_TILES, D_MODEL])
        rows_chan = sb("rows_chan", [P, 2, CAPACITY])
        rows_out = sb("rows_out", [P, 2, SLOT_TILES, D_MODEL])

        x1_chan = x_chan
        hidden = [t[:, :, :].rearrange("p a b -> p (a b)")[:, 0:HT * CAPACITY].rearrange("p (h s) -> p h s", h=HT)
                  for t in (u, dt)]
        picked = dtu[:, :, :].rearrange("p k (j d) -> p (k j) d", d=D_MODEL)

        psum = ctx.enter_context(nc.psum_tensor("psum", [P, 8, CH], F32))
        Y_BANK, A_BANK, B_BANK, C_BANK = 0, 4, 6, 7

        ident_made = sem("ident_made")
        consts_made = sem("consts_made")
        pads_made = sem("pads_made")
        x_loaded = [sem(f"x_loaded{q}") for q in range(NQ)]
        w_in_loaded = sem("w_in_loaded")
        vectors_loaded = sem("vectors_loaded")
        w_mid_loaded = sem("w_mid_loaded")
        w_late_loaded = sem("w_late_loaded")
        x_turned = sem("x_turned")
        x_chan_ready = sem("x_chan_ready")
        in_projected = sem("in_projected")
        x_in_ready = sem("x_in_ready")
        z_ready = sem("z_ready")
        conv_done = sem("conv_done")
        u_ready = sem("u_ready")
        bc_projected = sem("bc_projected")
        dt_projected = sem("dt_projected")
        bc_taken = sem("bc_taken")
        dt_raw_ready = sem("dt_raw_ready")
        soft_ready = sem("soft_ready")
        soft_step = sem("soft_step")
        dt_ready = sem("dt_ready")
        dtu_ready = sem("dtu_ready")
        w_x4_ready = sem("w_x4_ready")
        selector_ready = sem("selector_ready")
        a_ready = sem("a_ready")
        diag_ready = sem("diag_ready")
        dve_step = sem("dve_step")
        act_step = sem("act_step")
        gp_step = sem("gp_step")

        b_spread = sem("b_spread")
        c_spread = sem("c_spread")
        c_ready = sem("c_ready")
        drive_ready = sem("drive_ready")
        decay_ready = sem("decay_ready")
        scanned = sem("scanned")
        product_ready = sem("product_ready")
        summed = sem("summed")
        y_first_ready = sem("y_first_ready")

        gated = sem("gated")
        out_projected = sem("out_projected")
        residual_ready = sem("residual_ready")
        moments_ready = sem("moments_ready")
        rstd_ready = sem("rstd_ready")
        x1_ready = sem("x1_ready")
        x1_turned = sem("x1_turned")
        x1_chan_ready = sem("x1_chan_ready")
        logits_ready = sem("logits_ready")
        above_ready = sem("above_ready")
        exps_ready = sem("exps_ready")
        chosen_ready = sem("chosen_ready")
        ranks_counted = sem("ranks_counted")
        slots_ready = sem("slots_ready")
        zeros_made = sem("zeros_made")
        rows_cleared = sem("rows_cleared")
        scattered = sem("scattered")
        fc_loaded = [sem(f"fc_loaded{i}") for i in range(2)]
        proj_loaded = [sem(f"proj_loaded{i}") for i in range(2)]
        rows_loaded = [sem(f"rows_loaded{i}") for i in range(2)]
        rows_turned = sem("rows_turned")
        rows_chan_ready = sem("rows_chan_ready")
        fc_done = sem("fc_done")
        hidden_ready = sem("hidden_ready")
        proj_done = sem("proj_done")
        rows_out_ready = sem("rows_out_ready")
        rows_stored = [sem(f"rows_stored{i}") for i in range(2)]
        gathered = [sem(f"gathered{g}") for g in range(TPC)]
        combined = sem("combined")
        moments2_ready = sem("moments2_ready")
        rstd2_ready = sem("rstd2_ready")
        out_ready = sem("out_ready")
        out_stored = sem("out_stored")

        block = ctx.enter_context(nc.Block())
        x_rows = x.rearrange("b (j p) d -> p (b j) d", p=P)
        out_rows = out.rearrange("b (j p) d -> p (b j) d", p=P)
        LAST = BATCH * D_STATE - 1
        GROUPS = TILES // TPC

        @block.sync
        def _(sp):
            for q in range(NQ):
                sp.dma_start(x_tok[:, TPC * q:TPC * (q + 1), :], x_rows[:, TPC * q:TPC * (q + 1), :]).then_inc(x_loaded[q], 16)
                if q == 0:
                    sp.dma_start(w_in_sb[:, :], W_in).then_inc(w_in_loaded, 16)
            sp.dma_start(w_out_sb[:, :, :], W_out.rearrange("(t p) m -> p t m", p=P)).then_inc(w_late_loaded, 16)
            sp.dma_start(w_g_sb[:, :], w_g).then_inc(w_late_loaded, 16)
            sp.wait_ge(zeros_made, 1)
            cleared = slot_rows.rearrange("(g p r) d -> g p (r d)", g=8, p=P)
            for g in range(8):
                sp.dma_start(cleared[g], zeros[:, :]).then_inc(rows_cleared, 16)

            def load_weights(g, i):
                e = 2 * g + i
                sp.dma_start(fc_sb[:, i, :], c_fc[bass.ds(e, 1), :, :].rearrange("e p m -> p (e m)")).then_inc(fc_loaded[i], 16)
                sp.dma_start(proj_sb[:, i, :, :],
                             c_proj[bass.ds(e, 1), :, :].rearrange("e (h p) m -> p (e h) m", p=P)).then_inc(proj_loaded[i], 16)

            def load_rows(g, i):
                e = 2 * g + i
                sp.dma_start(rows_in[:, i, :, :],
                             slot_rows[bass.ds(e * CAPACITY, CAPACITY), :].rearrange("(s p) d -> p s d", p=P)).then_inc(rows_loaded[i], 16)

            def store_rows(g, i):
                e = 2 * g + i
                sp.wait_ge(rows_out_ready, e + 1)
                sp.dma_start(expert_rows[bass.ds(e * CAPACITY, CAPACITY), :].rearrange("(s p) d -> p s d", p=P),
                             rows_out[:, i, :, :]).then_inc(rows_stored[i], 16)

            for i in range(2):
                load_weights(0, i)
            sp.wait_ge(scattered, 16 * RUNS)
            for i in range(2):
                load_rows(0, i)
            with sp.Fori(1, PAIRS) as g:
                for i in range(2):
                    e = 2 * g + i
                    sp.wait_ge(rows_turned, e - 1)
                    load_rows(g, i)
                    sp.wait_ge(proj_done, e - 1)
                    load_weights(g, i)
                    store_rows(g - 1, i)
            for i in range(2):
                store_rows(PAIRS - 1, i)

            for g in range(GROUPS):
                sp.wait_ge(out_ready, g + 1)
                sp.dma_start(out_rows[:, TPC * g:TPC * (g + 1), :], x1[:, TPC * g:TPC * (g + 1), :]).then_inc(out_stored, 16)
            sp.wait_ge(out_stored, 16 * GROUPS)

        @block.tensor
        def _(pe):
            pe.wait_ge(ident_made, 2)

            def turn_x(q):
                pe.wait_ge(x_loaded[q], 16)
                if q:
                    pe.wait_ge(x_chan_ready, q)
                for j in range(TPC):
                    last = nc.tensor.transpose(psum[:, C_BANK, j * P:(j + 1) * P], x_tok[:, TPC * q + j, :], ident[:, :])
                last.then_inc(x_turned, 1)

            def project_in(q):
                pe.wait_ge(x_chan_ready, q + 1)
                for r in range(2 * DT):
                    if q and r < DT:
                        pe.wait_ge(x_in_ready, DT * (q - 1) + r + 1)
                    elif q:
                        pe.wait_ge(z_ready, DT * (q - 1) + r - DT + 1)
                    nc.tensor.matmul(psum[:, Y_BANK + r, :], w_in_sb[:, r * P:(r + 1) * P], x_chan[:, q * CH:(q + 1) * CH],
                                     start=True, stop=True).then_inc(in_projected, 1)

            def project_scan_inputs(q):
                pe.wait_ge(u_ready, DT * (q + 1))
                if q:
                    pe.wait_ge(bc_taken, q)
                for k in range(DT):
                    last = nc.tensor.matmul(psum[:, B_BANK, :], w_x4[:, k, :, :].rearrange("p a b -> p (a b)"),
                                            u[:, k, q * CH:(q + 1) * CH], start=(k == 0), stop=(k == DT - 1))
                last.then_inc(bc_projected, 1)
                for r in range(DT):
                    if q:
                        pe.wait_ge(dt_raw_ready, DT * (q - 1) + r + 1)
                    for k in range(DT):
                        last = nc.tensor.matmul(psum[:, A_BANK + r, :], w_dt_sb[:, k, r * P:(r + 1) * P],
                                                u[:, k, q * CH:(q + 1) * CH], start=(k == 0), stop=(k == DT - 1))
                    last.then_inc(dt_projected, 1)

            turn_x(0)
            pe.wait_ge(w_in_loaded, 16)
            for q in range(NQ):
                if q + 1 < NQ:
                    turn_x(q + 1)
                project_in(q)
                if q == 1:
                    pe.wait_ge(w_x4_ready, 1)
                if q:
                    project_scan_inputs(q - 1)
            project_scan_inputs(NQ - 1)

            def spread(i, b, c):
                n = i - D_STATE * b
                first = isinstance(i, int) and i == 0
                parts = bc_parts[:, b * SEQ + c * CH:b * SEQ + (c + 1) * CH]
                if not (first and c == 0):
                    pe.wait_ge(drive_ready, UNITS * i + DT * c)
                nc.tensor.matmul(psum[:, B_BANK, :], selector[:, bass.ds(n, 1), :].rearrange("p a b -> p (a b)"), parts,
                                 start=True, stop=True).then_inc(b_spread, 1)
                if not (first and c == 0):
                    pe.wait_ge(c_ready, NCH * i + c)
                nc.tensor.matmul(psum[:, C_BANK, :], selector[:, bass.ds(n + D_STATE, 1), :].rearrange("p a b -> p (a b)"), parts,
                                 start=True, stop=True).then_inc(c_spread, 1)

            def add_to_y(i, c):
                for d in range(DT):
                    pe.wait_ge(product_ready, UNITS * i + DT * c + d + 1)
                    nc.tensor.matmul(psum[:, Y_BANK + DT * c + d, :], ident[:, :], product[:, c, d, :],
                                     start=False, stop=True, skip_group_check=True).then_inc(summed, 1)

            def start_y(b):
                for c in range(NCH):
                    for d in range(DT):
                        t = b * SEQ + c * CH
                        nc.tensor.matmul(psum[:, Y_BANK + DT * c + d, :], diag_d[:, d, :], u[:, d, t:t + CH],
                                         start=True, stop=True, skip_group_check=True)

            pe.wait_ge(bc_taken, NQ)
            pe.wait_ge(x_chan_ready, NQ)
            pe.wait_ge(selector_ready, 1)
            pe.wait_ge(diag_ready, DT)
            pe.wait_ge(z_ready, DT * NQ)
            pe.wait_ge(x_in_ready, DT * NQ)
            for c in range(NCH):
                spread(0, 0, c)
            start_y(0)
            with pe.Fori(1, D_STATE) as i:
                for c in range(NCH):
                    spread(i, 0, c)
                    add_to_y(i - 1, c)
            for c in range(NCH):
                spread(D_STATE, 1, c)
                add_to_y(D_STATE - 1, c)
            pe.wait_ge(y_first_ready, UNITS)
            start_y(1)
            with pe.Fori(D_STATE + 1, 2 * D_STATE) as i:
                for c in range(NCH):
                    spread(i, 1, c)
                    add_to_y(i - 1, c)
            for c in range(NCH):
                add_to_y(LAST, c)

            pe.wait_ge(w_late_loaded, 32)
            pe.wait_ge(gated, BATCH * UNITS)
            for g in range(GROUPS):
                for j in range(TPC):
                    for k in range(DT):
                        t = (TPC * g + j) * P
                        last = nc.tensor.matmul(psum[:, Y_BANK + g, j * P:(j + 1) * P], z_gate[:, k, t:t + P], w_out_sb[:, k, :],
                                                start=(k == 0), stop=(k == DT - 1))
                last.then_inc(out_projected, 1)
            for g in range(GROUPS):
                pe.wait_ge(x1_ready, g + 1)
                for j in range(TPC):
                    last = nc.tensor.transpose(psum[:, A_BANK + g, j * P:(j + 1) * P], x1[:, TPC * g + j, :], ident[:, :])
                last.then_inc(x1_turned, 1)
            for g in range(GROUPS):
                pe.wait_ge(x1_chan_ready, g + 1)
                for j in range(TPC * g, TPC * (g + 1)):
                    last = nc.tensor.matmul(psum[:, Y_BANK, j * N_EXP:(j + 1) * N_EXP], x1_chan[:, j * P:(j + 1) * P], w_g_sb[:, :],
                                            start=True, stop=True)
            last.then_inc(logits_ready, 1)
            pe.wait_ge(chosen_ready, 1)
            marks = chosen_bf[:, :, :].rearrange("p r e -> p (r e)")
            nc.tensor.matmul(psum[:, Y_BANK + 1, 0:RUNS * N_EXP], upto[:, :], marks, start=True, stop=True)
            nc.tensor.matmul(psum[:, Y_BANK + 2, 0:RUNS * N_EXP], ones[:, :], marks, start=True, stop=True).then_inc(ranks_counted, 1)

            def turn_rows(g, i):
                e = 2 * g + i
                pe.wait_ge(rows_loaded[i], 16 * (g + 1))
                if not (isinstance(e, int) and e == 0):
                    pe.wait_ge(rows_chan_ready, e)
                for s in range(SLOT_TILES):
                    last = nc.tensor.transpose(psum[:, s // TPC, (s % TPC) * P:(s % TPC + 1) * P], rows_in[:, i, s, :], ident[:, :])
                last.then_inc(rows_turned, 1)

            def first_layer(g, i):
                e = 2 * g + i
                first = isinstance(e, int) and e == 0
                pe.wait_ge(fc_loaded[i], 16 * (g + 1))
                pe.wait_ge(rows_chan_ready, e + 1)
                for h in range(HT):
                    if not (first and h < 2):
                        pe.wait_ge(hidden_ready, HT * e + h - 1)
                    for s in range(2):
                        last = nc.tensor.matmul(psum[:, 2 + 2 * (h % 2) + s, 0:HALF], fc_sb[:, i, h * P:(h + 1) * P],
                                                rows_chan[:, i, s * HALF:(s + 1) * HALF], start=True, stop=True)
                    last.then_inc(fc_done, 1)

            def second_layer(g, i):
                e = 2 * g + i
                pe.wait_ge(proj_loaded[i], 16 * (g + 1))
                pe.wait_ge(hidden_ready, HT * (e + 1))
                if not (isinstance(e, int) and e == 0):
                    pe.wait_ge(rows_out_ready, e)
                for s in range(SLOT_TILES):
                    for h in range(HT):
                        last = nc.tensor.matmul(psum[:, 6 + s // TPC, (s % TPC) * P:(s % TPC + 1) * P], hidden[i][:, h, s * P:(s + 1) * P],
                                                proj_sb[:, i, h, :], start=(h == 0), stop=(h == HT - 1))
                last.then_inc(proj_done, 1)

            pe.wait_ge(slots_ready, 1)
            pe.wait_ge(x1_chan_ready, GROUPS)
            turn_rows(0, 0)
            first_layer(0, 0)
            turn_rows(0, 1)

            def expert_pair(g):
                first_layer(g, 1)
                turn_rows(g + 1, 0)
                second_layer(g, 0)
                first_layer(g + 1, 0)
                turn_rows(g + 1, 1)
                second_layer(g, 1)

            expert_pair(0)
            with pe.Fori(1, PAIRS - 1) as g:
                expert_pair(g)
            first_layer(PAIRS - 1, 1)
            second_layer(PAIRS - 1, 0)
            second_layer(PAIRS - 1, 1)

        @block.scalar
        def _(act):
            step = Tally()
            act.dma_start(channel_sb[:, :, :], channel_values).then_inc(vectors_loaded, 16)
            act.dma_start(a_log_sb[:, :], A_log.partition_broadcast(P)).then_inc(vectors_loaded, 16)
            act.dma_start(w_x_sb[:, :, :], W_x.rearrange("(t p) m -> p t m", p=P)).then_inc(w_mid_loaded, 16)
            act.dma_start(w_dt_sb[:, :, :], W_dt.rearrange("(t p) m -> p t m", p=P)).then_inc(w_mid_loaded, 16)

            def activate_u(q):
                for d in range(DT):
                    act.wait_ge(conv_done, DT * q + d + 1)
                    part = u[:, d, q * CH:(q + 1) * CH]
                    nc.scalar.activation(part, part, ACT.Silu).then_inc(u_ready, 1)

            for q in range(NQ):
                b, c = divmod(q, NCH)
                for d in range(DT):
                    act.wait_ge(in_projected, 2 * DT * q + d + 1)
                    nc.scalar.activation(x_in[:, d, b, PAD + c * CH:PAD + (c + 1) * CH], psum[:, Y_BANK + d, :],
                                         ACT.Copy).then_inc(x_in_ready, 1)
                for d in range(DT):
                    act.wait_ge(in_projected, 2 * DT * q + DT + d + 1)
                    nc.scalar.activation(z_gate[:, d, q * CH:(q + 1) * CH], psum[:, Y_BANK + DT + d, :],
                                         ACT.Silu).then_inc(z_ready, 1)
                if q:
                    activate_u(q - 1)
            activate_u(NQ - 1)

            act.preload_act_table_set("natural_log_exp_and_others")
            act.wait_ge(vectors_loaded, 16 * 2)
            nc.scalar.activation(a_exp[:, :], a_log_sb[:, :], ACT.Exp).then_inc(act_step, 1)
            act.wait_ge(act_step, step.up())
            for k in range(UNITS):
                nc.scalar.mul(a_neg[:, k, :], a_exp[:, :], -1.0).then_inc(a_ready, 1)
            for q in range(NQ):
                for d in range(DT):
                    k = DT * q + d
                    act.wait_ge(dt_raw_ready, k + 1)
                    if k >= 2:
                        act.wait_ge(dt_ready, k - 1)
                    nc.scalar.activation(soft[:, d, :], dt[:, d, q * CH:(q + 1) * CH], ACT.Abs).then_inc(act_step, 1)
                    step.up()
                first = step.n - DT
                for func, args in ((ACT.Exp, {"scale": -1.0}), (ACT.Ln, {"bias": 1.0})):
                    for d in range(DT):
                        act.wait_ge(act_step, first + d + 1)
                        done = act_step if func == ACT.Exp else soft_ready
                        nc.scalar.activation(soft[:, d, :], soft[:, d, :], func, **args).then_inc(done, 1)
                    if func == ACT.Exp:
                        first = step.n
                        step.up(DT)

            act.wait_ge(a_ready, UNITS)
            act.wait_ge(dt_ready, DT * NQ)

            def decays(i, b):
                n = i - D_STATE * b
                first = isinstance(i, int) and i == 0
                for c in range(NCH):
                    for d in range(DT):
                        if not (first and c == 0):
                            act.wait_ge(scanned, UNITS * i + DT * c + d - 1)
                        t = b * SEQ + c * CH
                        nc.scalar.activation(psum[:, A_BANK + d, :], dt[:, d, t:t + CH], ACT.Exp,
                                             scale=a_neg[:, DT * c + d, bass.ds(n, 1)]).then_inc(decay_ready, 1)
                    act.wait_ge(c_spread, NCH * i + c + 1)
                    if not first:
                        act.wait_ge(product_ready, UNITS * (i - 1) + DT * (c + 1))
                    nc.scalar.activation(c_wide[:, c, :], psum[:, C_BANK, :], ACT.Copy).then_inc(c_ready, 1)

            decays(0, 0)
            with act.Fori(1, D_STATE) as i:
                decays(i, 0)
            decays(D_STATE, 1)
            for c in range(NCH):
                for d in range(DT):
                    act.wait_ge(summed, UNITS * (D_STATE - 1) + DT * c + d + 1)
                    nc.scalar.activation(y_first[:, c, d, :], psum[:, Y_BANK + DT * c + d, :], ACT.Copy).then_inc(y_first_ready, 1)
            with act.Fori(D_STATE + 1, 2 * D_STATE) as i:
                decays(i, 1)

            def inverse_root(ready, done):
                act.wait_ge(ready, 1)
                nc.scalar.activation(log_var[:, :], moments[:, :, 1], ACT.Ln).then_inc(act_step, 1)
                act.wait_ge(act_step, step.up())
                nc.scalar.activation(rstd[:, :], log_var[:, :], ACT.Exp, scale=-0.5).then_inc(done, 1)

            inverse_root(moments_ready, rstd_ready)
            for g in range(GROUPS):
                act.wait_ge(x1_turned, g + 1)
                nc.scalar.activation(x1_chan[:, g * CH:(g + 1) * CH], psum[:, A_BANK + g, :], ACT.Copy).then_inc(x1_chan_ready, 1)
            act.wait_ge(above_ready, 1)
            nc.scalar.activation(exps[:, :, :], above[:, :, :], ACT.Exp).then_inc(exps_ready, 1)

            act.preload_act_table(ACT.Gelu)

            def activate_hidden(g, i):
                e = 2 * g + i
                first = isinstance(g, int) and g == 0
                if not first:
                    act.wait_ge(proj_done, e - 1)
                for h in range(HT):
                    act.wait_ge(fc_done, HT * e + h + 1)
                    nc.scalar.activation(hidden[i][:, h, :].rearrange("p (s k) -> p s k", s=2),
                                         psum[:, 2 + 2 * (h % 2):4 + 2 * (h % 2), 0:HALF], ACT.Gelu).then_inc(hidden_ready, 1)

            for i in range(2):
                activate_hidden(0, i)
            with act.Fori(1, PAIRS) as g:
                for i in range(2):
                    activate_hidden(g, i)

            act.preload_act_table_set("natural_log_exp_and_others")
            inverse_root(moments2_ready, rstd2_ready)

        @block.gpsimd
        def _(gp):
            step = Tally()
            nc.gpsimd.memset(ident[:, :], 0.0).then_inc(ident_made, 1)
            gp.wait_ge(ident_made, 1)
            nc.gpsimd.affine_select(out=ident[:, :], in_=ident[:, :], compare_op=ALU.not_equal, fill=1.0, base=0,
                                    pattern=[[-1, P]], channel_multiplier=1).then_inc(ident_made, 1)
            nc.gpsimd.memset(pick[:, :], 0.0).then_inc(gp_step, 1)
            for base in (0, 64, 96):
                gp.wait_ge(gp_step, step.up())
                nc.gpsimd.affine_select(out=pick[:, :], in_=pick[:, :], compare_op=ALU.not_equal, fill=1.0, base=-base,
                                        pattern=[[-1, 2 * D_STATE]], channel_multiplier=1).then_inc(gp_step, 1)
            gp.wait_ge(gp_step, step.up())
            nc.gpsimd.memset(upto[:, :], 1.0).then_inc(gp_step, 1)
            gp.wait_ge(gp_step, step.up())
            nc.gpsimd.affine_select(out=upto[:, :], in_=upto[:, :], compare_op=ALU.is_ge, fill=0.0, base=0,
                                    pattern=[[1, P]], channel_multiplier=-1).then_inc(gp_step, 1)
            nc.gpsimd.memset(ones[:, :], 1.0).then_inc(gp_step, 1)
            nc.gpsimd.iota(countdown[:, :], pattern=[[-1, N_EXP]], base=N_EXP, channel_multiplier=0,
                           allow_small_or_imprecise_dtypes=True).then_inc(gp_step, 1)
            nc.gpsimd.memset(run_keep[:, :, :], 1.0).then_inc(gp_step, 1)
            gp.wait_ge(gp_step, step.up(4))
            nc.gpsimd.memset(run_keep[:, :, 0:1], 0.0).then_inc(consts_made, 1)
            nc.gpsimd.memset(zeros[:, :], 0.0).then_inc(zeros_made, 1)

            for q in range(NQ):
                for d in range(DT):
                    gp.wait_ge(dt_ready, DT * q + d + 1)
                    at = slice(q * CH, (q + 1) * CH)
                    nc.gpsimd.tensor_tensor(dtu[:, d, at], dt[:, d, at], u[:, d, at], ALU.mult).then_inc(dtu_ready, 1)

            def products(i):
                first = isinstance(i, int) and i == 0
                for c in range(NCH):
                    gp.wait_ge(c_ready, NCH * i + c + 1)
                    for d in range(DT):
                        gp.wait_ge(scanned, UNITS * i + DT * c + d + 1)
                        if not first:
                            gp.wait_ge(summed, UNITS * (i - 1) + DT * c + d + 1)
                        nc.gpsimd.tensor_tensor(product[:, c, d, :], state[:, c, d, :], c_wide[:, c, :],
                                                ALU.mult).then_inc(product_ready, 1)

            products(0)
            with gp.Fori(1, BATCH * D_STATE) as i:
                products(i)

            gp.wait_ge(rows_cleared, 16 * 8)
            gp.wait_ge(slots_ready, 1)
            for r in range(RUNS):
                gp.indirect_dma_start(out=slot_rows, out_offset=bass.IndirectOffsetOnAxis(ap=scatter_at[:, r:r + 1], axis=0),
                                      in_=x1[:, r % TILES, :], in_offset=None, bounds_check=SLOTS - 1,
                                      oob_is_err=False).then_inc(scattered, 16)
            for i in range(2):
                gp.wait_ge(rows_stored[i], 16 * N_EXP // 2)
            for g in range(GROUPS):
                for k in range(TOP_K):
                    for j in range(TPC * g, TPC * (g + 1)):
                        r = k * TILES + j
                        gp.indirect_dma_start(out=picked[:, r, :], out_offset=None, in_=expert_rows,
                                              in_offset=bass.IndirectOffsetOnAxis(ap=gather_at[:, r:r + 1], axis=0),
                                              bounds_check=SLOTS - 1, oob_is_err=False).then_inc(gathered[g], 16)

        @block.vector
        def _(dve):
            step = Tally()
            for b in range(BATCH):
                nc.vector.memset(x_in[:, :, b, 0:PAD], 0.0).then_inc(pads_made, 1)

            def copy_x(q):
                dve.wait_ge(x_turned, q + 1)
                nc.vector.tensor_copy(x_chan[:, q * CH:(q + 1) * CH], psum[:, C_BANK, :]).then_inc(x_chan_ready, 1)

            def convolve(q):
                b, c = divmod(q, NCH)
                for d in range(DT):
                    dve.wait_ge(x_in_ready, DT * q + d + 1)
                    nc.vector.tensor_scalar(u[:, d, q * CH:(q + 1) * CH], x_in[:, d, b, c * CH:(c + 1) * CH],
                                            conv_w_sb[:, d, 0:1], conv_b_sb[:, d:d + 1], ALU.mult, ALU.add).then_inc(dve_step, 1)
                for k in range(1, D_CONV):
                    first = step.up(DT) - DT
                    for d in range(DT):
                        dve.wait_ge(dve_step, first + d + 1)
                        part = u[:, d, q * CH:(q + 1) * CH]
                        nc.vector.scalar_tensor_tensor(part, x_in[:, d, b, c * CH + k:(c + 1) * CH + k], conv_w_sb[:, d, k:k + 1], part,
                                                       ALU.mult, ALU.add).then_inc(conv_done if k == PAD else dve_step, 1)

            def take_scan_inputs(q):
                at = slice(q * CH, (q + 1) * CH)
                dve.wait_ge(bc_projected, q + 1)
                nc.vector.tensor_copy(bc_parts[:, at], psum[:, B_BANK, :]).then_inc(dve_step, 1)
                high_done = step.up()
                dve.wait_ge(dt_projected, DT * q + 1)
                nc.vector.tensor_scalar(dt[:, 0, at], psum[:, A_BANK, :], b_dt_sb[:, 0:1], None, ALU.add).then_inc(dt_raw_ready, 1)
                dve.wait_ge(dve_step, high_done)
                nc.vector.tensor_tensor(bc_rest[64:, :], psum[64:, B_BANK, :], bc_parts[64:, at], ALU.subtract).then_inc(dve_step, 1)
                rest_done = step.up()
                dve.wait_ge(dt_projected, DT * q + 2)
                nc.vector.tensor_scalar(dt[:, 1, at], psum[:, A_BANK + 1, :], b_dt_sb[:, 1:2], None, ALU.add).then_inc(dt_raw_ready, 1)
                dve.wait_ge(dve_step, rest_done)
                nc.vector.tensor_copy(bc_parts[64:, at], bc_rest[64:, :]).then_inc(dve_step, 1)
                dve.wait_ge(dve_step, step.up())
                nc.vector.tensor_tensor(bc_parts[96:, at], bc_rest[96:, :], bc_parts[96:, at], ALU.subtract).then_inc(bc_taken, 1)

            copy_x(0)
            dve.wait_ge(vectors_loaded, 16 * 2)
            dve.wait_ge(pads_made, BATCH)
            for q in range(NQ):
                if q + 1 < NQ:
                    copy_x(q + 1)
                convolve(q)
                if q == 0:
                    dve.wait_ge(w_mid_loaded, 32)
                    nc.vector.tensor_copy(w_x4[:, :, :, :], w_x_sb[:, :, :].unsqueeze(2).to_broadcast([P, DT, 4, 2 * D_STATE])).then_inc(w_x4_ready, 1)
                if q:
                    take_scan_inputs(q - 1)
            take_scan_inputs(NQ - 1)
            dve.wait_ge(ident_made, 2)
            dve.wait_ge(consts_made, 1)
            for d in range(DT):
                nc.vector.tensor_scalar(diag_d[:, d, :], ident[:, :], d_sb[:, d:d + 1], None, ALU.mult).then_inc(diag_ready, 1)
            nc.vector.tensor_copy(selector[:, :, :], pick[:, :].unsqueeze(2).to_broadcast([P, 2 * D_STATE, P])).then_inc(selector_ready, 1)
            for q in range(NQ):
                for d in range(DT):
                    dve.wait_ge(soft_ready, DT * q + d + 1)
                    part = dt[:, d, q * CH:(q + 1) * CH]
                    nc.vector.scalar_tensor_tensor(part, part, 0.0, soft[:, d, :], ALU.max, ALU.add).then_inc(dt_ready, 1)

            dve.wait_ge(dtu_ready, DT * NQ)

            def scans(i, b):
                first = isinstance(i, int) and i == 0
                for c in range(NCH):
                    t = b * SEQ + c * CH
                    dve.wait_ge(b_spread, NCH * i + c + 1)
                    for d in range(DT):
                        if not first:
                            dve.wait_ge(scanned, UNITS * (i - 1) + DT * c + d + 1)
                        nc.vector.tensor_tensor(drive[:, c, d, :], dtu[:, d, t:t + CH], psum[:, B_BANK, :],
                                                ALU.mult).then_inc(drive_ready, 1)
                    for d in range(DT):
                        unit = UNITS * i + DT * c + d
                        dve.wait_ge(decay_ready, unit + 1)
                        dve.wait_ge(drive_ready, unit + 1)
                        if not first:
                            dve.wait_ge(product_ready, unit - UNITS + 1)
                        if c:
                            dve.wait_ge(scanned, unit - DT + 1)
                        before = state[:, c - 1, d, CH - 1:CH] if c else 0.0
                        nc.vector.tensor_tensor_scan(state[:, c, d, :], psum[:, A_BANK + d, :], drive[:, c, d, :], before,
                                                     ALU.mult, ALU.add).then_inc(scanned, 1)

            scans(0, 0)
            for b in range(BATCH):
                with dve.Fori(max(1, D_STATE * b), D_STATE * (b + 1)) as i:
                    scans(i, b)

            for b in range(BATCH):
                for c in range(NCH):
                    for d in range(DT):
                        t = b * SEQ + c * CH
                        if b == 0:
                            dve.wait_ge(y_first_ready, DT * c + d + 1)
                        else:
                            dve.wait_ge(summed, UNITS * LAST + DT * c + d + 1)
                        y = y_first[:, c, d, :] if b == 0 else psum[:, Y_BANK + DT * c + d, :]
                        part = z_gate[:, d, t:t + CH]
                        nc.vector.tensor_tensor(part, part, y, ALU.mult).then_inc(gated, 1)

            def take_moments(rows, g):
                for j in range(TPC * g, TPC * (g + 1)):
                    nc.vector.bn_stats(stats[:, j, :], rows[:, j, :]).then_inc(dve_step, 1)
                first = step.up(TPC) - TPC
                for j in range(TPC):
                    dve.wait_ge(dve_step, first + j + 1)
                    nc.vector.bn_aggr(moments[:, TPC * g + j, :], stats[:, TPC * g + j, :]).then_inc(dve_step, 1)
                dve.wait_ge(dve_step, step.up(TPC))

            def add_eps(done):
                nc.vector.tensor_scalar(moments[:, :, 1], moments[:, :, 1], EPS, None, ALU.add).then_inc(dve_step, 1)
                dve.wait_ge(dve_step, step.up())
                nc.vector.tensor_copy(newton[:, :], moments[:, :, 1]).then_inc(done, 1)

            def refine(ready):
                dve.wait_ge(ready, 1)
                nc.vector.tensor_tensor(newton[:, :], rstd[:, :], rstd[:, :], ALU.mult).then_inc(dve_step, 1)
                dve.wait_ge(dve_step, step.up())
                nc.vector.tensor_tensor(newton[:, :], newton[:, :], moments[:, :, 1], ALU.mult).then_inc(dve_step, 1)
                dve.wait_ge(dve_step, step.up())
                nc.vector.tensor_scalar(newton[:, :], newton[:, :], -0.5, 1.5, ALU.mult, ALU.add).then_inc(dve_step, 1)
                dve.wait_ge(dve_step, step.up())
                nc.vector.tensor_tensor(rstd[:, :], rstd[:, :], newton[:, :], ALU.mult).then_inc(dve_step, 1)
                dve.wait_ge(dve_step, step.up())

            def normalize(g, done):
                for j in range(TPC * g, TPC * (g + 1)):
                    last = nc.vector.tensor_scalar(x1[:, j, :], x1[:, j, :], moments[:, j, 0:1], rstd[:, j:j + 1], ALU.subtract, ALU.mult)
                    last.then_inc(done if j == TPC * (g + 1) - 1 else dve_step, 1)
                step.up(TPC - 1)

            for g in range(GROUPS):
                dve.wait_ge(out_projected, g + 1)
                rows = x1[:, TPC * g:TPC * (g + 1), :]
                nc.vector.tensor_tensor(rows.rearrange("p j d -> p (j d)"), x_tok[:, TPC * g:TPC * (g + 1), :].rearrange("p j d -> p (j d)"),
                                        psum[:, Y_BANK + g, :], ALU.add).then_inc(residual_ready, 1)
                dve.wait_ge(residual_ready, g + 1)
                take_moments(x1, g)
            add_eps(moments_ready)
            refine(rstd_ready)
            for g in range(GROUPS):
                normalize(g, x1_ready)

            def chain(ins):
                ins.then_inc(dve_step, 1)
                dve.wait_ge(dve_step, step.up())

            key_row = countdown[:, :].unsqueeze(1).to_broadcast([P, TILES, N_EXP])
            dve.wait_ge(logits_ready, 1)
            chain(nc.vector.tensor_copy(logits[:, :, :].rearrange("p j e -> p (j e)"), psum[:, Y_BANK, 0:TILES * N_EXP]))
            source = logits
            for k in range(TOP_K):
                mark = chosen[:, k * TILES:(k + 1) * TILES, :]
                chain(nc.vector.tensor_reduce(top[:, k, :], source[:, :, :], axis=AX.X, op=ALU.max))
                chain(nc.vector.tensor_tensor(keys[:, :, :], source[:, :, :], top[:, k, :].unsqueeze(2).to_broadcast([P, TILES, N_EXP]), ALU.is_equal))
                chain(nc.vector.tensor_tensor(keys[:, :, :], keys[:, :, :], key_row, ALU.mult))
                chain(nc.vector.tensor_reduce(top_key[:, k, :], keys[:, :, :], axis=AX.X, op=ALU.max))
                chain(nc.vector.tensor_tensor(mark, key_row, top_key[:, k, :].unsqueeze(2).to_broadcast([P, TILES, N_EXP]), ALU.is_equal))
                if k == 0:
                    chain(nc.vector.scalar_tensor_tensor(logits2[:, :, :], mark, -BIG, logits[:, :, :], ALU.mult, ALU.add))
                    source = logits2
            nc.vector.tensor_copy(chosen_bf[:, :, :], chosen[:, :, :]).then_inc(chosen_ready, 1)
            chain(nc.vector.tensor_scalar(peak[:, :], top[:, 0, :], NEG_INF, None, ALU.max))
            for k in range(TOP_K):
                nc.vector.tensor_tensor(above[:, k, :], top[:, k, :], peak[:, :], ALU.subtract).then_inc(dve_step, 1)
            nc.vector.tensor_scalar(above[:, TOP_K, :], peak[:, :], -1.0, NEG_INF, ALU.mult, ALU.add).then_inc(dve_step, 1)
            dve.wait_ge(dve_step, step.up(TOP_K + 1))
            nc.vector.tensor_copy(denom[:, :], peak[:, :]).then_inc(above_ready, 1)
            dve.wait_ge(above_ready, 1)
            dve.wait_ge(exps_ready, 1)
            chain(nc.vector.tensor_tensor(denom[:, :], exps[:, 0, :], exps[:, 1, :], ALU.add))
            chain(nc.vector.scalar_tensor_tensor(denom[:, :], exps[:, TOP_K, :], float(N_EXP - TOP_K), denom[:, :], ALU.mult, ALU.add))
            chain(nc.vector.reciprocal(denom[:, :], denom[:, :]))
            for k in range(TOP_K):
                chain(nc.vector.tensor_tensor(weight[:, k * TILES:(k + 1) * TILES], exps[:, k, :], denom[:, :], ALU.mult))
            dve.wait_ge(ranks_counted, 1)
            counts = psum[:, Y_BANK + 2, 0:RUNS * N_EXP].rearrange("p (r e) -> p e r", e=N_EXP)
            chain(nc.vector.tensor_copy(run_totals[:, :, :], counts))
            flat = lambda a: a[:, :, :].rearrange("p a b -> p (a b)")
            chain(nc.vector.tensor_tensor_scan(flat(run_upto), flat(run_keep), flat(run_totals), 0.0, ALU.mult, ALU.add))
            chain(nc.vector.tensor_tensor(run_upto[:, :, :], run_upto[:, :, :], run_totals[:, :, :], ALU.subtract))
            inside = psum[:, Y_BANK + 1, 0:RUNS * N_EXP].rearrange("p (r e) -> p r e", e=N_EXP)
            chain(nc.vector.tensor_tensor(ranks[:, :, :], run_upto[:, :, :].rearrange("p e r -> p r e"), inside, ALU.add))
            chain(nc.vector.tensor_tensor(ranks[:, :, :], ranks[:, :, :], chosen[:, :, :], ALU.mult))
            chain(nc.vector.tensor_reduce(rank[:, :], ranks[:, :, :], axis=AX.X, op=ALU.add))
            chain(nc.vector.tensor_scalar(kept[:, :], rank[:, :], float(CAPACITY), None, ALU.is_le))
            chain(nc.vector.tensor_tensor(weight[:, :], weight[:, :], kept[:, :], ALU.mult))
            expert_key = top_key[:, :, :].rearrange("p k j -> p (k j)")
            chain(nc.vector.scalar_tensor_tensor(slot[:, :], expert_key, -float(CAPACITY), rank[:, :], ALU.mult, ALU.add))
            chain(nc.vector.tensor_scalar(slot[:, :], slot[:, :], float(SLOTS - 1), None, ALU.add))
            chain(nc.vector.tensor_tensor(slot_in[:, :], slot[:, :], kept[:, :], ALU.mult))
            chain(nc.vector.tensor_scalar(slot_out[:, :], kept[:, :], -float(4 * SLOTS), float(4 * SLOTS), ALU.mult, ALU.add))
            chain(nc.vector.tensor_tensor(slot_out[:, :], slot_out[:, :], slot_in[:, :], ALU.add))
            chain(nc.vector.tensor_copy(gather_at[:, :], slot_in[:, :]))
            nc.vector.tensor_copy(scatter_at[:, :], slot_out[:, :]).then_inc(slots_ready, 1)

            def copy_turned(g, i):
                e = 2 * g + i
                dve.wait_ge(rows_turned, e + 1)
                if not (isinstance(g, int) and g == 0):
                    dve.wait_ge(fc_done, HT * (e - 1))
                nc.vector.tensor_copy(rows_chan[:, i, 0:CH], psum[:, 0, :]).then_inc(dve_step, 1)
                nc.vector.tensor_copy(rows_chan[:, i, CH:CAPACITY], psum[:, 1, 0:CAPACITY - CH]).then_inc(rows_chan_ready, 1)

            def copy_results(g, i):
                e = 2 * g + i
                dve.wait_ge(proj_done, e + 1)
                if not (isinstance(g, int) and g == 0):
                    dve.wait_ge(rows_stored[i], 16 * g)
                flat_out = rows_out[:, i, :, :].rearrange("p s d -> p (s d)")
                nc.vector.tensor_copy(flat_out[:, 0:CH], psum[:, 6, :]).then_inc(dve_step, 1)
                nc.vector.tensor_copy(flat_out[:, CH:CAPACITY], psum[:, 7, 0:CAPACITY - CH]).then_inc(rows_out_ready, 1)

            for i in range(2):
                copy_turned(0, i)
            for i in range(2):
                copy_turned(1, i)
                copy_results(0, i)
            with dve.Fori(2, PAIRS) as g:
                for i in range(2):
                    copy_turned(g, i)
                    copy_results(g - 1, i)
            for i in range(2):
                copy_results(PAIRS - 1, i)
            step.up(2 * N_EXP)

            for g in range(GROUPS):
                dve.wait_ge(gathered[g], 16 * TOP_K * TPC)
                for k in range(TOP_K):
                    for j in range(TPC * g, TPC * (g + 1)):
                        r = k * TILES + j
                        nc.vector.scalar_tensor_tensor(x1[:, j, :], picked[:, r, :], weight[:, r:r + 1], x1[:, j, :],
                                                       ALU.mult, ALU.add).then_inc(dve_step, 1)
                    dve.wait_ge(dve_step, step.up(TPC))
                take_moments(x1, g)
            add_eps(moments2_ready)
            refine(rstd2_ready)
            for g in range(GROUPS):
                normalize(g, out_ready)


def kernel(L0_attn_x, L0_attn_W_in, L0_attn_conv_w, L0_attn_conv_b, L0_attn_W_x, L0_attn_W_dt, L0_attn_b_dt,
           L0_attn_A_log, L0_attn_D, L0_attn_W_out, L0_ffn_w_g, L0_ffn_c_fc, L0_ffn_c_proj):
    import concourse.bacc as bacc
    from concourse.bass_utils import run_bass_kernel_spmd

    columns = [np.asarray(a).reshape(D_INNER, -1) for a in (L0_attn_conv_w, L0_attn_conv_b, L0_attn_b_dt, L0_attn_D)]
    channel_values = np.concatenate(columns, axis=1).reshape(DT, P, D_CONV + 3).transpose(1, 0, 2)
    inputs = {"x": L0_attn_x, "W_in": L0_attn_W_in, "channel_values": channel_values, "W_x": L0_attn_W_x, "W_dt": L0_attn_W_dt,
              "A_log": L0_attn_A_log, "W_out": L0_attn_W_out, "w_g": L0_ffn_w_g, "c_fc": L0_ffn_c_fc, "c_proj": L0_ffn_c_proj}
    arrays = {f"in_{name}": np.ascontiguousarray(a) for name, a in inputs.items()}

    nc = bacc.Bacc("TRN2", target_bir_lowering=False, num_devices=1)
    args = [nc.dram_tensor(name, a.shape, mybir.dt.from_np(a.dtype), kind="ExternalInput").ap() for name, a in arrays.items()]
    args.append(nc.dram_tensor("out", (BATCH, SEQ, D_MODEL), F32, kind="ExternalOutput").ap())
    layer_program(nc, *args)
    result = run_bass_kernel_spmd(nc, [arrays], core_ids=[0])
    return result.results[0]["out"]
```

```python
from contextlib import ExitStack

import numpy as np

import concourse.bass as bass
from concourse import mybir
from concourse.alu_op_type import AluOpType as ALU

F32 = mybir.dt.float32
BF16 = mybir.dt.bfloat16
U32 = mybir.dt.uint32
ACT = mybir.ActivationFunctionType
AX = mybir.AxisListType

P = 128
BATCH, SEQ, D_MODEL = 2, 1024, 128
D_INNER, D_STATE, D_CONV = 256, 16, 4
TOKENS = BATCH * SEQ
DT = D_INNER // P
CH = 512
NCH = SEQ // CH
NQ = TOKENS // CH
TILES = TOKENS // P
TPC = CH // P
PAD = D_CONV - 1
N_EXP, TOP_K, D_HID = 8, 2, 512
HT = D_HID // P
NEG_INF = -1000000000.0
CAPACITY = int(TOP_K * 1.25 * TOKENS / N_EXP)
CAPACITY += CAPACITY % 2
SLOT_TILES = CAPACITY // P
assert SLOT_TILES * P == CAPACITY
SLOTS = N_EXP * CAPACITY
ROW = D_MODEL + 2
ROW_TO, ROW_WEIGHT = D_MODEL, D_MODEL + 1
RESULTS = TOP_K * TOKENS
NOWHERE = 4 * RESULTS
CLEARS = 8
PAIRS = N_EXP // 2
HALF = CAPACITY // 2
RUNS = TOP_K * TILES
EPS = 1e-05
UNITS = NCH * DT
BIG = 1e30


class Tally:

    def __init__(self):
        self.n = 0

    def up(self, k=1):
        self.n += k
        return self.n


def layer_program(nc, x, W_in, channel_values, W_x, W_dt, A_log, W_out, w_g, c_fc, c_proj, out):
    with ExitStack() as ctx:
        def sb(name, shape, dt=F32):
            return ctx.enter_context(nc.sbuf_tensor(name, shape, dt))

        def sem(name):
            return ctx.enter_context(nc.semaphore(name))

        slot_rows = nc.dram_tensor("slot_rows", [SLOTS, ROW], F32, kind="Internal").ap()
        result_rows = nc.dram_tensor("result_rows", [RESULTS, D_MODEL], F32, kind="Internal").ap()

        w_in_sb = sb("w_in_sb", [P, 2 * D_INNER])
        channel_sb = sb("channel_sb", [P, DT, D_CONV + 3])
        conv_w_sb = channel_sb[:, :, 0:D_CONV]
        conv_b_sb, b_dt_sb, d_sb = (channel_sb[:, :, D_CONV + k] for k in range(3))
        a_log_sb = sb("a_log_sb", [P, D_STATE])
        a_exp = sb("a_exp", [P, D_STATE])
        a_neg = sb("a_neg", [P, UNITS, D_STATE])
        w_x_sb = sb("w_x_sb", [P, DT, 2 * D_STATE])
        w_x4 = sb("w_x4", [P, DT, 4, 2 * D_STATE])
        w_dt_sb = sb("w_dt_sb", [P, DT, D_INNER])
        w_out_sb = sb("w_out_sb", [P, DT, D_MODEL])
        w_g_sb = sb("w_g_sb", [P, N_EXP])
        ident = sb("ident", [P, P])
        diag_d = sb("diag_d", [P, DT, P])
        pick = sb("pick", [P, 2 * D_STATE], BF16)
        selector = sb("selector", [P, 2 * D_STATE, P], BF16)
        upto = sb("upto", [P, P], BF16)
        ones = sb("ones", [P, P], BF16)
        blank = sb("blank", [P, SLOTS // P // CLEARS, ROW])
        zeros = sb("zeros", [P, RESULTS // P // CLEARS * D_MODEL])

        x_tok = sb("x_tok", [P, TILES, D_MODEL])
        x_chan = sb("x_chan", [P, TOKENS])
        x_in = sb("x_in", [P, DT, BATCH, PAD + SEQ])
        z_gate = sb("z_gate", [P, DT, TOKENS])
        u = sb("u", [P, DT, TOKENS])
        dt = sb("dt", [P, DT, TOKENS])
        dtu = sb("dtu", [P, DT, TOKENS])
        bc_parts = sb("bc_parts", [P, TOKENS], BF16)
        bc_rest = sb("bc_rest", [P, CH])
        soft = sb("soft", [P, 2, DT, CH])

        drive = sb("drive", [P, NCH, DT, CH])
        state = sb("state", [P, NCH, DT, CH])
        product = sb("product", [P, NCH, DT, CH])
        c_wide = sb("c_wide", [P, NCH, CH])
        y_first = sb("y_first", [P, NCH, DT, CH])

        sent = sb("sent", [P, TOP_K, TILES, ROW])
        x1 = sent[:, 0, :, 0:D_MODEL]
        final = x_tok
        stats = sb("stats", [P, TILES, 6])
        moments = sb("moments", [P, TILES, 2])
        log_var = sb("log_var", [P, TILES])
        rstd = sb("rstd", [P, TILES])
        newton = sb("newton", [P, TILES])
        countdown = sb("countdown", [P, N_EXP])
        logits = sb("logits", [P, TILES, N_EXP])
        logits2 = sb("logits2", [P, TILES, N_EXP])
        keys = sb("keys", [P, TILES, N_EXP])
        top = sb("top", [P, TOP_K, TILES])
        top_key = sb("top_key", [P, TOP_K, TILES])
        chosen = sb("chosen", [P, RUNS, N_EXP])
        chosen_bf = sb("chosen_bf", [P, RUNS, N_EXP], BF16)
        peak = sb("peak", [P, TILES])
        above = sb("above", [P, TOP_K + 1, TILES])
        exps = sb("exps", [P, TOP_K + 1, TILES])
        denom = sb("denom", [P, TILES])
        weight = sb("weight", [P, RUNS])
        run_totals = sb("run_totals", [P, N_EXP, RUNS])
        run_keep = sb("run_keep", [P, N_EXP, RUNS])
        run_upto = sb("run_upto", [P, N_EXP, RUNS])
        ranks = sb("ranks", [P, RUNS, N_EXP])
        rank = sb("rank", [P, RUNS])
        kept = sb("kept", [P, RUNS])
        slot = sb("slot", [P, RUNS])
        slot_out = sb("slot_out", [P, RUNS])
        slot_in = sb("slot_in", [P, RUNS])
        scatter_at = sb("scatter_at", [P, RUNS], U32)

        fc_sb = sb("fc_sb", [P, 2, D_HID])
        proj_sb = sb("proj_sb", [P, 2, HT, D_MODEL])
        rows_in = sb("rows_in", [P, 2, SLOT_TILES, ROW])
        tags = sb("tags", [P, N_EXP, SLOT_TILES, 2])
        result_at = sb("result_at", [P, 2, SLOT_TILES], U32)
        result_weight = sb("result_weight", [P, 2, SLOT_TILES])

        x1_chan = x_chan
        hidden = [t[:, :, :].rearrange("p a b -> p (a b)")[:, 0:HT * CAPACITY].rearrange("p (h s) -> p h s", h=HT)
                  for t in (u, dt)]
        rows_chan = product[:, :, :, :].rearrange("p a b c -> p a (b c)")[:, :, 0:CAPACITY]
        rows_out = state[:, :, :, :].rearrange("p a b (j d) -> p a (b j) d", d=D_MODEL)[:, :, 0:SLOT_TILES, :]
        results = dtu[:, :, :].rearrange("p k (j d) -> p (k j) d", d=D_MODEL)

        psum = ctx.enter_context(nc.psum_tensor("psum", [P, 8, CH], F32))
        Y_BANK, A_BANK, B_BANK, C_BANK = 0, 4, 6, 7

        ident_made = sem("ident_made")
        consts_made = sem("consts_made")
        pads_made = sem("pads_made")
        x_loaded = [sem(f"x_loaded{q}") for q in range(NQ)]
        w_in_loaded = sem("w_in_loaded")
        vectors_loaded = sem("vectors_loaded")
        w_mid_loaded = sem("w_mid_loaded")
        w_late_loaded = sem("w_late_loaded")
        x_turned = sem("x_turned")
        x_chan_ready = sem("x_chan_ready")
        in_projected = sem("in_projected")
        x_in_ready = sem("x_in_ready")
        z_ready = sem("z_ready")
        conv_done = sem("conv_done")
        u_ready = sem("u_ready")
        bc_projected = sem("bc_projected")
        dt_projected = sem("dt_projected")
        bc_taken = sem("bc_taken")
        dt_raw_ready = sem("dt_raw_ready")
        soft_ready = sem("soft_ready")
        soft_step = sem("soft_step")
        dt_ready = sem("dt_ready")
        dtu_ready = sem("dtu_ready")
        w_x4_ready = sem("w_x4_ready")
        selector_ready = sem("selector_ready")
        a_ready = sem("a_ready")
        diag_ready = sem("diag_ready")
        dve_step = sem("dve_step")
        act_step = sem("act_step")
        gp_step = sem("gp_step")

        b_spread = sem("b_spread")
        c_spread = sem("c_spread")
        c_ready = sem("c_ready")
        drive_ready = sem("drive_ready")
        decay_ready = sem("decay_ready")
        scanned = sem("scanned")
        product_ready = sem("product_ready")
        summed = sem("summed")
        y_first_ready = sem("y_first_ready")

        gated = sem("gated")
        out_projected = sem("out_projected")
        residual_ready = sem("residual_ready")
        moments_ready = sem("moments_ready")
        rstd_ready = sem("rstd_ready")
        x1_ready = sem("x1_ready")
        x1_turned = sem("x1_turned")
        x1_chan_ready = sem("x1_chan_ready")
        logits_ready = sem("logits_ready")
        above_ready = sem("above_ready")
        exps_ready = sem("exps_ready")
        chosen_ready = sem("chosen_ready")
        ranks_counted = sem("ranks_counted")
        logits_copied = sem("logits_copied")
        ranks_taken = sem("ranks_taken")
        slots_ready = sem("slots_ready")
        blanks_made = sem("blanks_made")
        rows_cleared = sem("rows_cleared")
        scattered = sem("scattered")
        fc_loaded = [sem(f"fc_loaded{i}") for i in range(2)]
        proj_loaded = [sem(f"proj_loaded{i}") for i in range(2)]
        rows_loaded = [sem(f"rows_loaded{i}") for i in range(2)]
        rows_turned = sem("rows_turned")
        rows_chan_ready = sem("rows_chan_ready")
        fc_done = sem("fc_done")
        hidden_ready = sem("hidden_ready")
        proj_done = sem("proj_done")
        rows_out_ready = sem("rows_out_ready")
        tags_copied = sem("tags_copied")
        result_tagged = sem("result_tagged")
        results_sent = [sem(f"results_sent{i}") for i in range(2)]
        results_loaded = [sem(f"results_loaded{g}") for g in range(NQ)]
        sent_copied = sem("sent_copied")
        sent_tagged = sem("sent_tagged")
        moments2_ready = sem("moments2_ready")
        rstd2_ready = sem("rstd2_ready")
        out_ready = sem("out_ready")
        out_stored = sem("out_stored")

        block = ctx.enter_context(nc.Block())
        x_rows = x.rearrange("b (j p) d -> p (b j) d", p=P)
        out_rows = out.rearrange("b (j p) d -> p (b j) d", p=P)
        LAST = BATCH * D_STATE - 1
        GROUPS = TILES // TPC
        HALF_TILES = TILES // BATCH

        @block.sync
        def _(sp):
            for q in range(NQ):
                sp.dma_start(x_tok[:, TPC * q:TPC * (q + 1), :], x_rows[:, TPC * q:TPC * (q + 1), :]).then_inc(x_loaded[q], 16)
                if q == 0:
                    sp.dma_start(w_in_sb[:, :], W_in).then_inc(w_in_loaded, 16)
            sp.dma_start(w_out_sb[:, :, :], W_out.rearrange("(t p) m -> p t m", p=P)).then_inc(w_late_loaded, 16)
            sp.dma_start(w_g_sb[:, :], w_g).then_inc(w_late_loaded, 16)
            sp.wait_ge(blanks_made, 2)
            blank_slots = slot_rows.rearrange("(g p r) d -> g p (r d)", g=CLEARS, p=P)
            blank_results = result_rows.rearrange("(g p r) d -> g p (r d)", g=CLEARS, p=P)
            for g in range(CLEARS):
                sp.dma_start(blank_slots[g], blank[:, :, :].rearrange("p r d -> p (r d)")).then_inc(rows_cleared, 16)
                sp.dma_start(blank_results[g], zeros[:, :]).then_inc(rows_cleared, 16)

            def load_first(g, i):
                sp.dma_start(fc_sb[:, i, :], c_fc[bass.ds(2 * g + i, 1), :, :].rearrange("e p m -> p (e m)")).then_inc(fc_loaded[i], 16)

            def load_second(g, i):
                sp.dma_start(proj_sb[:, i, :, :],
                             c_proj[bass.ds(2 * g + i, 1), :, :].rearrange("e (h p) m -> p (e h) m", p=P)).then_inc(proj_loaded[i], 16)

            def load_rows(g, i):
                sp.dma_start(rows_in[:, i, :, :],
                             slot_rows[bass.ds((2 * g + i) * CAPACITY, CAPACITY), :].rearrange("(s p) d -> p s d", p=P)).then_inc(rows_loaded[i], 16)

            for i in range(2):
                load_first(0, i)
                load_second(0, i)
            sp.wait_ge(scattered, 16 * RUNS)
            for i in range(2):
                load_rows(0, i)
            with sp.Fori(1, PAIRS) as g:
                for i in range(2):
                    e = 2 * g + i
                    sp.wait_ge(rows_turned, e - 1)
                    sp.wait_ge(tags_copied, e - 1)
                    load_rows(g, i)
                    sp.wait_ge(fc_done, HT * (e - 1))
                    load_first(g, i)
                    sp.wait_ge(proj_done, e - 1)
                    load_second(g, i)

            for i in range(2):
                sp.wait_ge(results_sent[i], 16 * SLOT_TILES * PAIRS)
            in_order = result_rows.rearrange("(k j p) d -> p (k j) d", k=TOP_K, p=P)
            for g in range(GROUPS):
                for k in range(TOP_K):
                    at = slice(k * TILES + TPC * g, k * TILES + TPC * (g + 1))
                    sp.dma_start(results[:, at, :], in_order[:, at, :]).then_inc(results_loaded[g], 16)

            for g in range(GROUPS):
                sp.wait_ge(out_ready, TPC * (g + 1))
                sp.dma_start(out_rows[:, TPC * g:TPC * (g + 1), :], final[:, TPC * g:TPC * (g + 1), :]).then_inc(out_stored, 16)
            sp.wait_ge(out_stored, 16 * GROUPS)

        @block.tensor
        def _(pe):
            pe.wait_ge(ident_made, 2)

            def turn_x(q):
                pe.wait_ge(x_loaded[q], 16)
                if q:
                    pe.wait_ge(x_chan_ready, q)
                for j in range(TPC):
                    last = nc.tensor.transpose(psum[:, C_BANK, j * P:(j + 1) * P], x_tok[:, TPC * q + j, :], ident[:, :])
                last.then_inc(x_turned, 1)

            def project_in(q):
                pe.wait_ge(x_chan_ready, q + 1)
                for r in range(2 * DT):
                    if q and r < DT:
                        pe.wait_ge(x_in_ready, DT * (q - 1) + r + 1)
                    elif q:
                        pe.wait_ge(z_ready, DT * (q - 1) + r - DT + 1)
                    nc.tensor.matmul(psum[:, Y_BANK + r, :], w_in_sb[:, r * P:(r + 1) * P], x_chan[:, q * CH:(q + 1) * CH],
                                     start=True, stop=True).then_inc(in_projected, 1)

            def project_scan_inputs(q):
                pe.wait_ge(u_ready, DT * (q + 1))
                if q:
                    pe.wait_ge(bc_taken, q)
                for k in range(DT):
                    last = nc.tensor.matmul(psum[:, B_BANK, :], w_x4[:, k, :, :].rearrange("p a b -> p (a b)"),
                                            u[:, k, q * CH:(q + 1) * CH], start=(k == 0), stop=(k == DT - 1))
                last.then_inc(bc_projected, 1)
                for r in range(DT):
                    if q:
                        pe.wait_ge(dt_raw_ready, DT * (q - 1) + r + 1)
                    for k in range(DT):
                        last = nc.tensor.matmul(psum[:, A_BANK + r, :], w_dt_sb[:, k, r * P:(r + 1) * P],
                                                u[:, k, q * CH:(q + 1) * CH], start=(k == 0), stop=(k == DT - 1))
                    last.then_inc(dt_projected, 1)

            turn_x(0)
            pe.wait_ge(w_in_loaded, 16)
            for q in range(NQ):
                if q + 1 < NQ:
                    turn_x(q + 1)
                project_in(q)
                if q == 1:
                    pe.wait_ge(w_x4_ready, 1)
                if q:
                    project_scan_inputs(q - 1)
            project_scan_inputs(NQ - 1)

            def spread(i, b, c):
                n = i - D_STATE * b
                first = isinstance(i, int) and i == 0
                parts = bc_parts[:, b * SEQ + c * CH:b * SEQ + (c + 1) * CH]
                if not (first and c == 0):
                    pe.wait_ge(drive_ready, UNITS * i + DT * c)
                nc.tensor.matmul(psum[:, B_BANK, :], selector[:, bass.ds(n, 1), :].rearrange("p a b -> p (a b)"), parts,
                                 start=True, stop=True).then_inc(b_spread, 1)
                if not (first and c == 0):
                    pe.wait_ge(c_ready, NCH * i + c)
                nc.tensor.matmul(psum[:, C_BANK, :], selector[:, bass.ds(n + D_STATE, 1), :].rearrange("p a b -> p (a b)"), parts,
                                 start=True, stop=True).then_inc(c_spread, 1)

            def add_to_y(i, c):
                for d in range(DT):
                    pe.wait_ge(product_ready, UNITS * i + DT * c + d + 1)
                    nc.tensor.matmul(psum[:, Y_BANK + DT * c + d, :], ident[:, :], product[:, c, d, :],
                                     start=False, stop=True, skip_group_check=True).then_inc(summed, 1)

            def start_y(b):
                for c in range(NCH):
                    for d in range(DT):
                        t = b * SEQ + c * CH
                        nc.tensor.matmul(psum[:, Y_BANK + DT * c + d, :], diag_d[:, d, :], u[:, d, t:t + CH],
                                         start=True, stop=True, skip_group_check=True)

            pe.wait_ge(bc_taken, NQ)
            pe.wait_ge(x_chan_ready, NQ)
            pe.wait_ge(selector_ready, 1)
            pe.wait_ge(diag_ready, DT)
            pe.wait_ge(z_ready, DT * NQ)
            pe.wait_ge(x_in_ready, DT * NQ)
            for c in range(NCH):
                spread(0, 0, c)
            start_y(0)
            with pe.Fori(1, D_STATE) as i:
                for c in range(NCH):
                    spread(i, 0, c)
                    add_to_y(i - 1, c)
            for c in range(NCH):
                spread(D_STATE, 1, c)
                add_to_y(D_STATE - 1, c)
            pe.wait_ge(y_first_ready, UNITS)
            start_y(1)
            with pe.Fori(D_STATE + 1, 2 * D_STATE) as i:
                for c in range(NCH):
                    spread(i, 1, c)
                    add_to_y(i - 1, c)
            for c in range(NCH):
                add_to_y(LAST, c)

            OUT_BANKS = [B_BANK, C_BANK, Y_BANK, Y_BANK + 1]
            pe.wait_ge(w_late_loaded, 32)

            def project_out(g):
                pe.wait_ge(gated, DT * (g + 1))
                for j in range(TPC):
                    for k in range(DT):
                        t = (TPC * g + j) * P
                        last = nc.tensor.matmul(psum[:, OUT_BANKS[g], j * P:(j + 1) * P], z_gate[:, k, t:t + P], w_out_sb[:, k, :],
                                                start=(k == 0), stop=(k == DT - 1))
                last.then_inc(out_projected, 1)

            def turn_x1(g):
                pe.wait_ge(x1_ready, TPC * (g + 1))
                for j in range(TPC):
                    last = nc.tensor.transpose(psum[:, A_BANK + g % 2, j * P:(j + 1) * P], x1[:, TPC * g + j, :], ident[:, :])
                last.then_inc(x1_turned, 1)

            def make_logits(b):
                for g in range(NCH * b, NCH * (b + 1)):
                    pe.wait_ge(x1_chan_ready, g + 1)
                    for j in range(TPC * g, TPC * (g + 1)):
                        last = nc.tensor.matmul(psum[:, Y_BANK + 2, j * N_EXP:(j + 1) * N_EXP], x1_chan[:, j * P:(j + 1) * P], w_g_sb[:, :],
                                                start=True, stop=True)
                last.then_inc(logits_ready, 1)

            def count_choices(first, last, done):
                marks = chosen_bf[:, first:last, :].rearrange("p r e -> p (r e)")
                at = slice(first * N_EXP, last * N_EXP)
                pe.wait_ge(chosen_ready, done)
                nc.tensor.matmul(psum[:, Y_BANK + 3, at], upto[:, :], marks, start=True, stop=True)
                nc.tensor.matmul(psum[:, A_BANK, at], ones[:, :], marks, start=True, stop=True).then_inc(ranks_counted, 1)

            pe.wait_ge(drive_ready, UNITS * (LAST + 1))
            pe.wait_ge(c_ready, NCH * (LAST + 1))
            project_out(0)
            project_out(1)
            pe.wait_ge(gated, BATCH * UNITS)
            project_out(2)
            project_out(3)
            pe.wait_ge(scanned, UNITS * (LAST + 1))
            turn_x1(0)
            turn_x1(1)
            make_logits(0)
            pe.wait_ge(logits_copied, 1)
            count_choices(0, HALF_TILES, 1)
            pe.wait_ge(ranks_taken, 1)
            turn_x1(2)
            turn_x1(3)
            make_logits(1)
            pe.wait_ge(x1_chan_ready, GROUPS)
            pe.wait_ge(logits_copied, 2)
            count_choices(HALF_TILES, RUNS, 2)

            def turn_rows(g, i):
                e = 2 * g + i
                pe.wait_ge(rows_loaded[i], 16 * (g + 1))
                if not (isinstance(e, int) and e == 0):
                    pe.wait_ge(rows_chan_ready, e)
                for s in range(SLOT_TILES):
                    last = nc.tensor.transpose(psum[:, s // TPC, (s % TPC) * P:(s % TPC + 1) * P], rows_in[:, i, s, 0:D_MODEL], ident[:, :])
                last.then_inc(rows_turned, 1)

            def first_layer(g, i):
                e = 2 * g + i
                first = isinstance(e, int) and e == 0
                pe.wait_ge(fc_loaded[i], 16 * (g + 1))
                pe.wait_ge(rows_chan_ready, e + 1)
                for h in range(HT):
                    if not (first and h < 2):
                        pe.wait_ge(hidden_ready, HT * e + h - 1)
                    for s in range(2):
                        last = nc.tensor.matmul(psum[:, 2 + 2 * (h % 2) + s, 0:HALF], fc_sb[:, i, h * P:(h + 1) * P],
                                                rows_chan[:, i, s * HALF:(s + 1) * HALF], start=True, stop=True)
                    last.then_inc(fc_done, 1)

            def second_layer(g, i):
                e = 2 * g + i
                pe.wait_ge(proj_loaded[i], 16 * (g + 1))
                pe.wait_ge(hidden_ready, HT * (e + 1))
                if not (isinstance(e, int) and e == 0):
                    pe.wait_ge(rows_out_ready, e)
                for s in range(SLOT_TILES):
                    for h in range(HT):
                        last = nc.tensor.matmul(psum[:, 6 + s // TPC, (s % TPC) * P:(s % TPC + 1) * P], hidden[i][:, h, s * P:(s + 1) * P],
                                                proj_sb[:, i, h, :], start=(h == 0), stop=(h == HT - 1))
                last.then_inc(proj_done, 1)

            pe.wait_ge(ranks_taken, 2)
            turn_rows(0, 0)
            first_layer(0, 0)
            turn_rows(0, 1)

            def expert_pair(g):
                first_layer(g, 1)
                turn_rows(g + 1, 0)
                second_layer(g, 0)
                first_layer(g + 1, 0)
                turn_rows(g + 1, 1)
                second_layer(g, 1)

            expert_pair(0)
            with pe.Fori(1, PAIRS - 1) as g:
                expert_pair(g)
            first_layer(PAIRS - 1, 1)
            second_layer(PAIRS - 1, 0)
            second_layer(PAIRS - 1, 1)

        @block.scalar
        def _(act):
            step = Tally()
            act.dma_start(channel_sb[:, :, :], channel_values).then_inc(vectors_loaded, 16)
            act.dma_start(a_log_sb[:, :], A_log.partition_broadcast(P)).then_inc(vectors_loaded, 16)
            act.dma_start(w_x_sb[:, :, :], W_x.rearrange("(t p) m -> p t m", p=P)).then_inc(w_mid_loaded, 16)
            act.dma_start(w_dt_sb[:, :, :], W_dt.rearrange("(t p) m -> p t m", p=P)).then_inc(w_mid_loaded, 16)

            def activate_u(q):
                for d in range(DT):
                    act.wait_ge(conv_done, DT * q + d + 1)
                    part = u[:, d, q * CH:(q + 1) * CH]
                    nc.scalar.activation(part, part, ACT.Silu).then_inc(u_ready, 1)

            def add_dt_bias(q):
                for d in range(DT):
                    act.wait_ge(dt_projected, DT * q + d + 1)
                    nc.scalar.activation(dt[:, d, q * CH:(q + 1) * CH], psum[:, A_BANK + d, :], ACT.Identity,
                                         bias=b_dt_sb[:, d:d + 1]).then_inc(dt_raw_ready, 1)

            act.wait_ge(vectors_loaded, 16 * 2)
            for q in range(NQ):
                b, c = divmod(q, NCH)
                for d in range(DT):
                    act.wait_ge(in_projected, 2 * DT * q + d + 1)
                    nc.scalar.activation(x_in[:, d, b, PAD + c * CH:PAD + (c + 1) * CH], psum[:, Y_BANK + d, :],
                                         ACT.Copy).then_inc(x_in_ready, 1)
                for d in range(DT):
                    act.wait_ge(in_projected, 2 * DT * q + DT + d + 1)
                    nc.scalar.activation(z_gate[:, d, q * CH:(q + 1) * CH], psum[:, Y_BANK + DT + d, :],
                                         ACT.Silu).then_inc(z_ready, 1)
                if q:
                    activate_u(q - 1)
                if q > 1:
                    add_dt_bias(q - 2)
            activate_u(NQ - 1)
            add_dt_bias(NQ - 2)

            act.preload_act_table_set("natural_log_exp_and_others")
            nc.scalar.activation(a_exp[:, :], a_log_sb[:, :], ACT.Exp).then_inc(act_step, 1)
            act.wait_ge(act_step, step.up())
            for k in range(UNITS):
                nc.scalar.mul(a_neg[:, k, :], a_exp[:, :], -1.0).then_inc(a_ready, 1)

            def softplus(q):
                for d in range(DT):
                    k = DT * q + d
                    act.wait_ge(dt_raw_ready, k + 1)
                    if k >= 2 * DT:
                        act.wait_ge(dt_ready, k - 2 * DT + 1)
                    nc.scalar.activation(soft[:, q % 2, d, :], dt[:, d, q * CH:(q + 1) * CH], ACT.Abs).then_inc(act_step, 1)
                    step.up()
                first = step.n - DT
                for func, args in ((ACT.Exp, {"scale": -1.0}), (ACT.Ln, {"bias": 1.0})):
                    for d in range(DT):
                        act.wait_ge(act_step, first + d + 1)
                        done = act_step if func == ACT.Exp else soft_ready
                        nc.scalar.activation(soft[:, q % 2, d, :], soft[:, q % 2, d, :], func, **args).then_inc(done, 1)
                    if func == ACT.Exp:
                        first = step.n
                        step.up(DT)

            for q in range(NCH):
                softplus(q)
            add_dt_bias(NQ - 1)

            act.wait_ge(a_ready, UNITS)
            act.wait_ge(dt_ready, DT * NCH)
            act.wait_ge(dt_raw_ready, DT * NQ)

            def decays(i, b):
                n = i - D_STATE * b
                first = isinstance(i, int) and i == 0
                for c in range(NCH):
                    for d in range(DT):
                        if not (first and c == 0):
                            act.wait_ge(scanned, UNITS * i + DT * c + d - 1)
                        t = b * SEQ + c * CH
                        nc.scalar.activation(psum[:, A_BANK + d, :], dt[:, d, t:t + CH], ACT.Exp,
                                             scale=a_neg[:, DT * c + d, bass.ds(n, 1)]).then_inc(decay_ready, 1)
                    act.wait_ge(c_spread, NCH * i + c + 1)
                    if not first:
                        act.wait_ge(product_ready, UNITS * (i - 1) + DT * (c + 1))
                    nc.scalar.activation(c_wide[:, c, :], psum[:, C_BANK, :], ACT.Copy).then_inc(c_ready, 1)

            decays(0, 0)
            for q in range(NCH, NQ):
                softplus(q)
            with act.Fori(1, D_STATE) as i:
                decays(i, 0)
            act.wait_ge(dt_ready, DT * NQ)
            decays(D_STATE, 1)
            for c in range(NCH):
                for d in range(DT):
                    act.wait_ge(summed, UNITS * (D_STATE - 1) + DT * c + d + 1)
                    nc.scalar.activation(y_first[:, c, d, :], psum[:, Y_BANK + DT * c + d, :], ACT.Copy).then_inc(y_first_ready, 1)
            with act.Fori(D_STATE + 1, 2 * D_STATE) as i:
                decays(i, 1)

            def inverse_root(tiles, ready, value, done):
                act.wait_ge(ready, value)
                nc.scalar.activation(log_var[:, tiles], moments[:, tiles, 1], ACT.Ln).then_inc(act_step, 1)
                act.wait_ge(act_step, step.up())
                nc.scalar.activation(rstd[:, tiles], log_var[:, tiles], ACT.Exp, scale=-0.5).then_inc(done, 1)

            for b in range(BATCH):
                half = slice(HALF_TILES * b, HALF_TILES * (b + 1))
                inverse_root(half, moments_ready, b + 1, rstd_ready)
                for g in range(NCH * b, NCH * (b + 1)):
                    act.wait_ge(x1_turned, g + 1)
                    nc.scalar.activation(x1_chan[:, g * CH:(g + 1) * CH], psum[:, A_BANK + g % 2, :], ACT.Copy).then_inc(x1_chan_ready, 1)
                    tiles = slice(TPC * g, TPC * (g + 1))
                    nc.scalar.activation(sent[:, 1, tiles, 0:D_MODEL], sent[:, 0, tiles, 0:D_MODEL], ACT.Copy).then_inc(sent_copied, 1)
                act.wait_ge(above_ready, b + 1)
                nc.scalar.activation(exps[:, :, half], above[:, :, half], ACT.Exp).then_inc(exps_ready, 1)

            act.preload_act_table(ACT.Gelu)

            def activate_hidden(g, i):
                e = 2 * g + i
                first = isinstance(g, int) and g == 0
                if not first:
                    act.wait_ge(proj_done, e - 1)
                for h in range(HT):
                    act.wait_ge(fc_done, HT * e + h + 1)
                    nc.scalar.activation(hidden[i][:, h, :].rearrange("p (s k) -> p s k", s=2),
                                         psum[:, 2 + 2 * (h % 2):4 + 2 * (h % 2), 0:HALF], ACT.Gelu).then_inc(hidden_ready, 1)

            for i in range(2):
                activate_hidden(0, i)
            with act.Fori(1, PAIRS) as g:
                for i in range(2):
                    activate_hidden(g, i)

            act.preload_act_table_set("natural_log_exp_and_others")
            for g in range(GROUPS):
                inverse_root(slice(TPC * g, TPC * (g + 1)), moments2_ready, g + 1, rstd2_ready)

        @block.gpsimd
        def _(gp):
            step = Tally()
            nc.gpsimd.memset(ident[:, :], 0.0).then_inc(ident_made, 1)
            gp.wait_ge(ident_made, 1)
            nc.gpsimd.affine_select(out=ident[:, :], in_=ident[:, :], compare_op=ALU.not_equal, fill=1.0, base=0,
                                    pattern=[[-1, P]], channel_multiplier=1).then_inc(ident_made, 1)
            nc.gpsimd.memset(pick[:, :], 0.0).then_inc(gp_step, 1)
            for base in (0, 64, 96):
                gp.wait_ge(gp_step, step.up())
                nc.gpsimd.affine_select(out=pick[:, :], in_=pick[:, :], compare_op=ALU.not_equal, fill=1.0, base=-base,
                                        pattern=[[-1, 2 * D_STATE]], channel_multiplier=1).then_inc(gp_step, 1)
            gp.wait_ge(gp_step, step.up())
            nc.gpsimd.memset(upto[:, :], 1.0).then_inc(gp_step, 1)
            gp.wait_ge(gp_step, step.up())
            nc.gpsimd.affine_select(out=upto[:, :], in_=upto[:, :], compare_op=ALU.is_ge, fill=0.0, base=0,
                                    pattern=[[1, P]], channel_multiplier=-1).then_inc(gp_step, 1)
            nc.gpsimd.memset(ones[:, :], 1.0).then_inc(gp_step, 1)
            nc.gpsimd.iota(countdown[:, :], pattern=[[-1, N_EXP]], base=N_EXP, channel_multiplier=0,
                           allow_small_or_imprecise_dtypes=True).then_inc(gp_step, 1)
            nc.gpsimd.memset(run_keep[:, :, :], 1.0).then_inc(gp_step, 1)
            gp.wait_ge(gp_step, step.up(4))
            nc.gpsimd.memset(run_keep[:, :, 0:1], 0.0).then_inc(consts_made, 1)
            nc.gpsimd.memset(blank[:, :, :], 0.0).then_inc(gp_step, 1)
            gp.wait_ge(gp_step, step.up())
            nc.gpsimd.memset(blank[:, :, ROW_TO:ROW_TO + 1], float(NOWHERE)).then_inc(blanks_made, 1)
            nc.gpsimd.memset(zeros[:, :], 0.0).then_inc(blanks_made, 1)
            nc.gpsimd.iota(sent[:, :, :, ROW_TO], pattern=[[TOKENS, TOP_K], [P, TILES]], base=0, channel_multiplier=1,
                           allow_small_or_imprecise_dtypes=True).then_inc(sent_tagged, 1)
            gp.wait_ge(vectors_loaded, 16 * 2)
            for d in range(DT):
                nc.gpsimd.tensor_tensor(diag_d[:, d, :], ident[:, :], d_sb[:, d:d + 1].to_broadcast([P, P]), ALU.mult).then_inc(diag_ready, 1)
            nc.gpsimd.tensor_copy(selector[:, :, :], pick[:, :].unsqueeze(2).to_broadcast([P, 2 * D_STATE, P])).then_inc(selector_ready, 1)

            def times_u(q):
                for d in range(DT):
                    gp.wait_ge(dt_ready, DT * q + d + 1)
                    at = slice(q * CH, (q + 1) * CH)
                    nc.gpsimd.tensor_tensor(dtu[:, d, at], dt[:, d, at], u[:, d, at], ALU.mult).then_inc(dtu_ready, 1)

            for q in range(NCH):
                times_u(q)

            def products(i):
                first = isinstance(i, int) and i == 0
                for c in range(NCH):
                    gp.wait_ge(c_ready, NCH * i + c + 1)
                    gp.wait_ge(scanned, UNITS * i + DT * (c + 1))
                    if not first:
                        gp.wait_ge(summed, UNITS * (i - 1) + DT * (c + 1))
                    nc.gpsimd.tensor_tensor(product[:, c, :, :], state[:, c, :, :],
                                            c_wide[:, c, :].unsqueeze(1).to_broadcast([P, DT, CH]), ALU.mult).then_inc(product_ready, DT)

            products(0)
            for q in range(NCH, NQ):
                times_u(q)
            with gp.Fori(1, BATCH * D_STATE) as i:
                products(i)

            gp.wait_ge(rows_cleared, 16 * 2 * CLEARS)
            gp.wait_ge(sent_tagged, 1)

            def scatter(r):
                gp.indirect_dma_start(out=slot_rows, out_offset=bass.IndirectOffsetOnAxis(ap=scatter_at[:, r:r + 1], axis=0),
                                      in_=sent[:, r // TILES, r % TILES, :], in_offset=None, bounds_check=SLOTS - 1,
                                      oob_is_err=False).then_inc(scattered, 16)

            gp.wait_ge(slots_ready, 1)
            for r in range(HALF_TILES):
                scatter(r)
            gp.wait_ge(slots_ready, 2)
            gp.wait_ge(sent_copied, GROUPS)
            for r in range(HALF_TILES, RUNS):
                scatter(r)
            for g in range(PAIRS):
                for i in range(2):
                    gp.wait_ge(rows_out_ready, 2 * g + i + 1)
                    for s in range(SLOT_TILES):
                        gp.indirect_dma_start(out=result_rows, out_offset=bass.IndirectOffsetOnAxis(ap=result_at[:, i, s:s + 1], axis=0),
                                              in_=rows_out[:, i, s, :], in_offset=None, bounds_check=RESULTS - 1,
                                              oob_is_err=False).then_inc(results_sent[i], 16)

        @block.vector
        def _(dve):
            step = Tally()
            for b in range(BATCH):
                nc.vector.memset(x_in[:, :, b, 0:PAD], 0.0).then_inc(pads_made, 1)

            def copy_x(q):
                dve.wait_ge(x_turned, q + 1)
                nc.vector.tensor_copy(x_chan[:, q * CH:(q + 1) * CH], psum[:, C_BANK, :]).then_inc(x_chan_ready, 1)

            def convolve(q):
                b, c = divmod(q, NCH)
                for d in range(DT):
                    dve.wait_ge(x_in_ready, DT * q + d + 1)
                    nc.vector.tensor_scalar(u[:, d, q * CH:(q + 1) * CH], x_in[:, d, b, c * CH:(c + 1) * CH],
                                            conv_w_sb[:, d, 0:1], conv_b_sb[:, d:d + 1], ALU.mult, ALU.add).then_inc(dve_step, 1)
                for k in range(1, D_CONV):
                    first = step.up(DT) - DT
                    for d in range(DT):
                        dve.wait_ge(dve_step, first + d + 1)
                        part = u[:, d, q * CH:(q + 1) * CH]
                        nc.vector.scalar_tensor_tensor(part, x_in[:, d, b, c * CH + k:(c + 1) * CH + k], conv_w_sb[:, d, k:k + 1], part,
                                                       ALU.mult, ALU.add).then_inc(conv_done if k == PAD else dve_step, 1)

            def take_scan_inputs(q):
                at = slice(q * CH, (q + 1) * CH)
                dve.wait_ge(bc_projected, q + 1)
                nc.vector.tensor_copy(bc_parts[:, at], psum[:, B_BANK, :]).then_inc(dve_step, 1)
                high_done = step.up()
                dve.wait_ge(dve_step, high_done)
                nc.vector.tensor_tensor(bc_rest[64:, :], psum[64:, B_BANK, :], bc_parts[64:, at], ALU.subtract).then_inc(dve_step, 1)
                rest_done = step.up()
                dve.wait_ge(dve_step, rest_done)
                nc.vector.tensor_copy(bc_parts[64:, at], bc_rest[64:, :]).then_inc(dve_step, 1)
                dve.wait_ge(dve_step, step.up())
                nc.vector.tensor_tensor(bc_parts[96:, at], bc_rest[96:, :], bc_parts[96:, at], ALU.subtract).then_inc(bc_taken, 1)

            copy_x(0)
            dve.wait_ge(vectors_loaded, 16 * 2)
            dve.wait_ge(pads_made, BATCH)
            for q in range(NQ):
                if q + 1 < NQ:
                    copy_x(q + 1)
                convolve(q)
                if q == 0:
                    dve.wait_ge(w_mid_loaded, 32)
                    nc.vector.tensor_copy(w_x4[:, :, :, :], w_x_sb[:, :, :].unsqueeze(2).to_broadcast([P, DT, 4, 2 * D_STATE])).then_inc(w_x4_ready, 1)
                if q:
                    take_scan_inputs(q - 1)
            take_scan_inputs(NQ - 1)
            def finish_dt(q):
                for d in range(DT):
                    dve.wait_ge(soft_ready, DT * q + d + 1)
                    part = dt[:, d, q * CH:(q + 1) * CH]
                    nc.vector.scalar_tensor_tensor(part, part, 0.0, soft[:, q % 2, d, :], ALU.max, ALU.add).then_inc(dt_ready, 1)

            for q in range(NCH):
                finish_dt(q)

            dve.wait_ge(dtu_ready, DT * NCH)

            def scans(i, b):
                first = isinstance(i, int) and i == 0
                for c in range(NCH):
                    t = b * SEQ + c * CH
                    dve.wait_ge(b_spread, NCH * i + c + 1)
                    if not first:
                        dve.wait_ge(scanned, UNITS * (i - 1) + DT * (c + 1))
                    nc.vector.tensor_tensor(drive[:, c, :, :], dtu[:, :, t:t + CH],
                                            psum[:, B_BANK, :].unsqueeze(1).to_broadcast([P, DT, CH]), ALU.mult).then_inc(drive_ready, DT)
                    for d in range(DT):
                        unit = UNITS * i + DT * c + d
                        dve.wait_ge(decay_ready, unit + 1)
                        dve.wait_ge(drive_ready, unit + 1)
                        if not first:
                            dve.wait_ge(product_ready, unit - UNITS + 1)
                        if c:
                            dve.wait_ge(scanned, unit - DT + 1)
                        before = state[:, c - 1, d, CH - 1:CH] if c else 0.0
                        nc.vector.tensor_tensor_scan(state[:, c, d, :], psum[:, A_BANK + d, :], drive[:, c, d, :], before,
                                                     ALU.mult, ALU.add).then_inc(scanned, 1)

            def gate(b, c):
                t = b * SEQ + c * CH
                for d in range(DT):
                    if b == 0:
                        dve.wait_ge(y_first_ready, DT * c + d + 1)
                        y = y_first[:, c, d, :]
                    else:
                        dve.wait_ge(summed, UNITS * LAST + DT * c + d + 1)
                        y = psum[:, Y_BANK + DT * c + d, :]
                    part = z_gate[:, d, t:t + CH]
                    nc.vector.tensor_tensor(part, part, y, ALU.mult).then_inc(gated, 1)

            scans(0, 0)
            for q in range(NCH, NQ):
                finish_dt(q)
            with dve.Fori(1, D_STATE) as i:
                scans(i, 0)
            dve.wait_ge(dtu_ready, DT * NQ)
            with dve.Fori(D_STATE, 2 * D_STATE - 1) as i:
                scans(i, 1)
            for c in range(NCH):
                gate(0, c)
            scans(LAST, 1)
            for c in range(NCH):
                gate(1, c)

            def take_moments(rows, g):
                tiles = slice(TPC * g, TPC * (g + 1))
                for j in range(TPC * g, TPC * (g + 1)):
                    nc.vector.bn_stats(stats[:, j, :], rows[:, j, :]).then_inc(dve_step, 1)
                first = step.up(TPC) - TPC
                for j in range(TPC):
                    dve.wait_ge(dve_step, first + j + 1)
                    nc.vector.bn_aggr(moments[:, TPC * g + j, :], stats[:, TPC * g + j, :]).then_inc(dve_step, 1)
                dve.wait_ge(dve_step, step.up(TPC))
                return nc.vector.tensor_scalar(moments[:, tiles, 1], moments[:, tiles, 1], EPS, None, ALU.add)

            def refine(tiles, ready, value):
                dve.wait_ge(ready, value)
                nc.vector.tensor_tensor(newton[:, tiles], rstd[:, tiles], rstd[:, tiles], ALU.mult).then_inc(dve_step, 1)
                dve.wait_ge(dve_step, step.up())
                nc.vector.tensor_tensor(newton[:, tiles], newton[:, tiles], moments[:, tiles, 1], ALU.mult).then_inc(dve_step, 1)
                dve.wait_ge(dve_step, step.up())
                nc.vector.tensor_scalar(newton[:, tiles], newton[:, tiles], -0.5, 1.5, ALU.mult, ALU.add).then_inc(dve_step, 1)
                dve.wait_ge(dve_step, step.up())
                nc.vector.tensor_tensor(rstd[:, tiles], rstd[:, tiles], newton[:, tiles], ALU.mult).then_inc(dve_step, 1)
                dve.wait_ge(dve_step, step.up())

            def normalize(rows, g, done):
                for j in range(TPC * g, TPC * (g + 1)):
                    nc.vector.tensor_scalar(rows[:, j, :], rows[:, j, :], moments[:, j, 0:1], rstd[:, j:j + 1],
                                            ALU.subtract, ALU.mult).then_inc(done, 1)

            def first_norm_moments(g):
                tiles = slice(TPC * g, TPC * (g + 1))
                bank = [B_BANK, C_BANK, Y_BANK, Y_BANK + 1][g]
                dve.wait_ge(out_projected, g + 1)
                nc.vector.tensor_tensor(x1[:, tiles, :], x_tok[:, tiles, :],
                                        psum[:, bank, :].rearrange("p (j d) -> p j d", d=D_MODEL), ALU.add).then_inc(residual_ready, 1)
                dve.wait_ge(residual_ready, g + 1)
                take_moments(x1, g).then_inc(moments_ready if g % NCH else dve_step, 1)
                if g % NCH == 0:
                    dve.wait_ge(dve_step, step.up())

            def first_norm(b):
                refine(slice(HALF_TILES * b, HALF_TILES * (b + 1)), rstd_ready, b + 1)
                for g in range(NCH * b, NCH * (b + 1)):
                    normalize(x1, g, x1_ready)

            def chain(ins):
                ins.then_inc(dve_step, 1)
                dve.wait_ge(dve_step, step.up())

            shape = [P, HALF_TILES, N_EXP]
            key_row = countdown[:, :].unsqueeze(1).to_broadcast(shape)

            def choose(b):
                half = slice(HALF_TILES * b, HALF_TILES * (b + 1))
                dve.wait_ge(logits_ready, b + 1)
                nc.vector.tensor_copy(logits[:, half, :],
                                      psum[:, Y_BANK + 2, HALF_TILES * N_EXP * b:HALF_TILES * N_EXP * (b + 1)].rearrange(
                                          "p (j e) -> p j e", e=N_EXP)).then_inc(logits_copied, 1)
                dve.wait_ge(logits_copied, b + 1)
                source = logits
                for k in range(TOP_K):
                    mark = chosen[:, k * TILES + HALF_TILES * b:k * TILES + HALF_TILES * (b + 1), :]
                    chain(nc.vector.tensor_reduce(top[:, k, half], source[:, half, :], axis=AX.X, op=ALU.max))
                    chain(nc.vector.tensor_tensor(keys[:, half, :], source[:, half, :], top[:, k, half].unsqueeze(2).to_broadcast(shape), ALU.is_equal))
                    chain(nc.vector.tensor_tensor(keys[:, half, :], keys[:, half, :], key_row, ALU.mult))
                    chain(nc.vector.tensor_reduce(top_key[:, k, half], keys[:, half, :], axis=AX.X, op=ALU.max))
                    chain(nc.vector.tensor_tensor(mark, key_row, top_key[:, k, half].unsqueeze(2).to_broadcast(shape), ALU.is_equal))
                    if k == 0:
                        chain(nc.vector.scalar_tensor_tensor(logits2[:, half, :], mark, -BIG, logits[:, half, :], ALU.mult, ALU.add))
                        source = logits2
                if b == 0:
                    nc.vector.tensor_copy(chosen_bf[:, 0:HALF_TILES, :], chosen[:, 0:HALF_TILES, :]).then_inc(chosen_ready, 1)
                else:
                    nc.vector.tensor_copy(chosen_bf[:, HALF_TILES:RUNS, :], chosen[:, HALF_TILES:RUNS, :]).then_inc(chosen_ready, 1)
                chain(nc.vector.tensor_scalar(peak[:, half], top[:, 0, half], NEG_INF, None, ALU.max))
                chain(nc.vector.tensor_scalar(above[:, TOP_K, half], peak[:, half], -1.0, NEG_INF, ALU.mult, ALU.add))
                nc.vector.tensor_tensor(above[:, 0:TOP_K, half], top[:, :, half], peak[:, half].unsqueeze(1).to_broadcast([P, TOP_K, HALF_TILES]),
                                        ALU.subtract).then_inc(above_ready, 1)
                dve.wait_ge(exps_ready, b + 1)
                chain(nc.vector.tensor_tensor(denom[:, half], exps[:, 0, half], exps[:, 1, half], ALU.add))
                chain(nc.vector.scalar_tensor_tensor(denom[:, half], exps[:, TOP_K, half], float(N_EXP - TOP_K), denom[:, half], ALU.mult, ALU.add))
                chain(nc.vector.reciprocal(denom[:, half], denom[:, half]))
                chain(nc.vector.tensor_tensor(weight[:, :].rearrange("p (k j) -> p k j", k=TOP_K)[:, :, half], exps[:, 0:TOP_K, half],
                                              denom[:, half].unsqueeze(1).to_broadcast([P, TOP_K, HALF_TILES]), ALU.mult))

            sent_weight = sent[:, :, :, ROW_WEIGHT].rearrange("p k j -> p (k j)")
            expert_key = top_key[:, :, :].rearrange("p k j -> p (k j)")

            def place(first, last, done):
                runs, n = slice(first, last), last - first
                dve.wait_ge(ranks_counted, done)
                dve.wait_ge(consts_made, 1)
                at = slice(first * N_EXP, last * N_EXP)
                chain(nc.vector.tensor_copy(run_totals[:, :, runs], psum[:, A_BANK, at].rearrange("p (r e) -> p e r", e=N_EXP)))
                if first == 0:
                    chain(nc.vector.memset(run_totals[:, :, last:RUNS], 0.0))
                flat = lambda a: a[:, :, :].rearrange("p a b -> p (a b)")
                chain(nc.vector.tensor_tensor_scan(flat(run_upto), flat(run_keep), flat(run_totals), 0.0, ALU.mult, ALU.add))
                chain(nc.vector.tensor_tensor(run_upto[:, :, runs], run_upto[:, :, runs], run_totals[:, :, runs], ALU.subtract))
                nc.vector.tensor_tensor(ranks[:, runs, :], run_upto[:, :, runs].rearrange("p e r -> p r e"),
                                        psum[:, Y_BANK + 3, at].rearrange("p (r e) -> p r e", e=N_EXP), ALU.add).then_inc(ranks_taken, 1)
                dve.wait_ge(ranks_taken, done)
                chain(nc.vector.tensor_tensor(ranks[:, runs, :], ranks[:, runs, :], chosen[:, runs, :], ALU.mult))
                chain(nc.vector.tensor_reduce(rank[:, runs], ranks[:, runs, :], axis=AX.X, op=ALU.add))
                chain(nc.vector.tensor_scalar(kept[:, runs], rank[:, runs], float(CAPACITY), None, ALU.is_le))
                nc.vector.tensor_tensor(sent_weight[:, runs], weight[:, runs], kept[:, runs], ALU.mult).then_inc(dve_step, 1)
                nc.vector.scalar_tensor_tensor(slot[:, runs], expert_key[:, runs], -float(CAPACITY), rank[:, runs], ALU.mult, ALU.add).then_inc(dve_step, 1)
                nc.vector.tensor_scalar(slot_out[:, runs], kept[:, runs], -float(4 * SLOTS), float(5 * SLOTS - 1), ALU.mult, ALU.add).then_inc(dve_step, 1)
                dve.wait_ge(dve_step, step.up(3))
                nc.vector.tensor_tensor(scatter_at[:, runs], slot[:, runs], slot_out[:, runs], ALU.add).then_inc(slots_ready, 1)

            first_norm_moments(0)
            first_norm_moments(1)
            first_norm(0)
            first_norm_moments(2)
            first_norm_moments(3)
            choose(0)
            place(0, HALF_TILES, 1)
            first_norm(1)
            choose(1)
            place(HALF_TILES, RUNS, 2)

            def copy_turned(g, i):
                e = 2 * g + i
                dve.wait_ge(rows_turned, e + 1)
                nc.vector.tensor_scalar(tags[:, bass.ds(e, 1), :, :].rearrange("p a s k -> p (a s) k"),
                                        rows_in[:, i, :, ROW_TO:ROW], 1.0, None, ALU.mult).then_inc(tags_copied, 1)
                if not (isinstance(g, int) and g == 0):
                    dve.wait_ge(fc_done, HT * (e - 1))
                nc.vector.tensor_copy(rows_chan[:, i, :], psum[:, 0:2, :].rearrange("p b c -> p (b c)")[:, 0:CAPACITY]).then_inc(rows_chan_ready, 1)

            def copy_results(g, i):
                e = 2 * g + i
                if not (isinstance(g, int) and g == 0):
                    dve.wait_ge(results_sent[i], 16 * SLOT_TILES * g)
                dve.wait_ge(tags_copied, e + 1)
                tag = tags[:, bass.ds(e, 1), :, :].rearrange("p a s k -> p (a s) k")
                nc.vector.tensor_scalar(result_at[:, i, :], tag[:, :, 0], 1.0, None, ALU.mult).then_inc(result_tagged, 1)
                nc.vector.tensor_scalar(result_weight[:, i, :], tag[:, :, 1], 1.0, None, ALU.mult).then_inc(result_tagged, 1)
                dve.wait_ge(result_tagged, 2 * (e + 1))
                dve.wait_ge(proj_done, e + 1)
                nc.vector.tensor_tensor(rows_out[:, i, :, :],
                                        psum[:, 6:8, :].rearrange("p b (j d) -> p (b j) d", d=D_MODEL)[:, 0:SLOT_TILES, :],
                                        result_weight[:, i, :].unsqueeze(2).to_broadcast([P, SLOT_TILES, D_MODEL]),
                                        ALU.mult).then_inc(rows_out_ready, 1)

            for i in range(2):
                copy_turned(0, i)
            for i in range(2):
                copy_turned(1, i)
                copy_results(0, i)
            with dve.Fori(2, PAIRS) as g:
                for i in range(2):
                    copy_turned(g, i)
                    copy_results(g - 1, i)
            for i in range(2):
                copy_results(PAIRS - 1, i)

            for g in range(GROUPS):
                tiles = slice(TPC * g, TPC * (g + 1))
                dve.wait_ge(results_loaded[g], 16 * TOP_K)
                chain(nc.vector.tensor_tensor(final[:, tiles, :], x1[:, tiles, :], results[:, tiles, :], ALU.add))
                chain(nc.vector.tensor_tensor(final[:, tiles, :], final[:, tiles, :],
                                              results[:, TILES + TPC * g:TILES + TPC * (g + 1), :], ALU.add))
                take_moments(final, g).then_inc(moments2_ready, 1)
                if g:
                    refine(slice(TPC * (g - 1), TPC * g), rstd2_ready, g)
                    normalize(final, g - 1, out_ready)
            refine(slice(TPC * (GROUPS - 1), TILES), rstd2_ready, GROUPS)
            normalize(final, GROUPS - 1, out_ready)


def kernel(L0_attn_x, L0_attn_W_in, L0_attn_conv_w, L0_attn_conv_b, L0_attn_W_x, L0_attn_W_dt, L0_attn_b_dt,
           L0_attn_A_log, L0_attn_D, L0_attn_W_out, L0_ffn_w_g, L0_ffn_c_fc, L0_ffn_c_proj):
    import concourse.bacc as bacc
    from concourse.bass_utils import run_bass_kernel_spmd

    columns = [np.asarray(a).reshape(D_INNER, -1) for a in (L0_attn_conv_w, L0_attn_conv_b, L0_attn_b_dt, L0_attn_D)]
    channel_values = np.concatenate(columns, axis=1).reshape(DT, P, D_CONV + 3).transpose(1, 0, 2)
    inputs = {"x": L0_attn_x, "W_in": L0_attn_W_in, "channel_values": channel_values, "W_x": L0_attn_W_x, "W_dt": L0_attn_W_dt,
              "A_log": L0_attn_A_log, "W_out": L0_attn_W_out, "w_g": L0_ffn_w_g, "c_fc": L0_ffn_c_fc, "c_proj": L0_ffn_c_proj}
    arrays = {f"in_{name}": np.ascontiguousarray(a) for name, a in inputs.items()}

    nc = bacc.Bacc("TRN2", target_bir_lowering=False, num_devices=1)
    args = [nc.dram_tensor(name, a.shape, mybir.dt.from_np(a.dtype), kind="ExternalInput").ap() for name, a in arrays.items()]
    args.append(nc.dram_tensor("out", (BATCH, SEQ, D_MODEL), F32, kind="ExternalOutput").ap())
    layer_program(nc, *args)
    result = run_bass_kernel_spmd(nc, [arrays], core_ids=[0])
    return result.results[0]["out"]
```

```python
from contextlib import ExitStack

import numpy as np

import concourse.bass as bass
from concourse import mybir
from concourse.alu_op_type import AluOpType as ALU

F32 = mybir.dt.float32
BF16 = mybir.dt.bfloat16
U32 = mybir.dt.uint32
ACT = mybir.ActivationFunctionType
AX = mybir.AxisListType

P = 128
BATCH, SEQ, D_MODEL = 2, 1024, 128
D_INNER, D_STATE, D_CONV = 256, 16, 4
TOKENS = BATCH * SEQ
DT = D_INNER // P
CH = 512
NCH = SEQ // CH
NQ = TOKENS // CH
TILES = TOKENS // P
TPC = CH // P
PAD = D_CONV - 1
N_EXP, TOP_K, D_HID = 8, 2, 512
HT = D_HID // P
NEG_INF = -1000000000.0
CAPACITY = int(TOP_K * 1.25 * TOKENS / N_EXP)
CAPACITY += CAPACITY % 2
SLOT_TILES = CAPACITY // P
assert SLOT_TILES * P == CAPACITY
SLOTS = N_EXP * CAPACITY
ROW = D_MODEL + 2
ROW_TO, ROW_WEIGHT = D_MODEL, D_MODEL + 1
RESULTS = TOP_K * TOKENS
NOWHERE = 4 * RESULTS
CLEARS = 8
PAIRS = N_EXP // 2
HALF = CAPACITY // 2
RUNS = TOP_K * TILES
EPS = 1e-05
UNITS = NCH * DT


class Tally:

    def __init__(self):
        self.n = 0

    def up(self, k=1):
        self.n += k
        return self.n


def layer_program(nc, x, W_in, channel_values, W_x, W_dt, A_log, W_out, w_g, c_fc, c_proj, out):
    with ExitStack() as ctx:
        def sb(name, shape, dt=F32):
            return ctx.enter_context(nc.sbuf_tensor(name, shape, dt))

        def sem(name):
            return ctx.enter_context(nc.semaphore(name))

        slot_rows = nc.dram_tensor("slot_rows", [SLOTS, ROW], F32, kind="Internal").ap()
        result_rows = nc.dram_tensor("result_rows", [RESULTS, D_MODEL], F32, kind="Internal").ap()

        w_in_sb = sb("w_in_sb", [P, 2 * D_INNER])
        channel_sb = sb("channel_sb", [P, DT, D_CONV + 3])
        conv_w_sb = channel_sb[:, :, 0:D_CONV]
        conv_b_sb, b_dt_sb, d_sb = (channel_sb[:, :, D_CONV + k] for k in range(3))
        a_log_sb = sb("a_log_sb", [P, D_STATE])
        a_exp = sb("a_exp", [P, D_STATE])
        a_neg = sb("a_neg", [P, UNITS, D_STATE])
        w_x_sb = sb("w_x_sb", [P, DT, 2 * D_STATE])
        w_x4 = sb("w_x4", [P, DT, 4, 2 * D_STATE])
        w_dt_sb = sb("w_dt_sb", [P, DT, D_INNER])
        w_out_sb = sb("w_out_sb", [P, DT, D_MODEL])
        w_g_sb = sb("w_g_sb", [P, N_EXP])
        ident = sb("ident", [P, P])
        diag_d = sb("diag_d", [P, DT, P])
        pick = sb("pick", [P, 2 * D_STATE], BF16)
        selector = sb("selector", [P, 2 * D_STATE, P], BF16)
        upto = sb("upto", [P, P], BF16)
        ones = sb("ones", [P, P], BF16)
        ones_wide = sb("ones_wide", [P, P])
        w_g_sum = sb("w_g_sum", [P, N_EXP])
        blank = sb("blank", [P, SLOTS // P // CLEARS, ROW])
        zeros = sb("zeros", [P, RESULTS // P // CLEARS * D_MODEL])

        x_tok = sb("x_tok", [P, TILES, D_MODEL])
        x_chan = sb("x_chan", [P, TOKENS])
        x_in = sb("x_in", [P, DT, BATCH, PAD + SEQ])
        z_gate = sb("z_gate", [P, DT, TOKENS])
        u = sb("u", [P, DT, TOKENS])
        dt = sb("dt", [P, DT, TOKENS])
        dtu = sb("dtu", [P, DT, TOKENS])
        bc_parts = sb("bc_parts", [P, TOKENS], BF16)
        bc_rest = sb("bc_rest", [P, CH])
        soft = sb("soft", [P, 2, DT, CH])

        drive = sb("drive", [P, NCH, DT, CH])
        state = sb("state", [P, NCH, DT, CH])
        product = sb("product", [P, NCH, DT, CH])
        c_wide = sb("c_wide", [P, NCH, CH])
        y_first = sb("y_first", [P, NCH, DT, CH])

        sent = sb("sent", [P, TOP_K, TILES, ROW])
        x1 = sent[:, 0, :, 0:D_MODEL]
        final = x_tok
        stats = sb("stats", [P, TILES, 6])
        moments = sb("moments", [P, TILES, 2])
        log_var = sb("log_var", [P, TILES])
        rstd = sb("rstd", [P, TILES])
        newton = sb("newton", [P, TILES])
        expert_number = sb("expert_number", [P, N_EXP])
        logits = sb("logits", [P, TILES, N_EXP])
        shift = sb("shift", [P, TILES])
        mean_logits = sb("mean_logits", [P, TILES // BATCH, N_EXP])
        sorted_logits = sb("sorted_logits", [P, TILES, N_EXP])
        sorted_experts = sb("sorted_experts", [P, TILES, N_EXP], U32)
        expert = sb("expert", [P, TOP_K, TILES])
        chosen = sb("chosen", [P, BATCH, TOP_K, TILES // BATCH, N_EXP], BF16)
        peak = sb("peak", [P, TILES])
        above = sb("above", [P, TOP_K + 1, TILES])
        exps = sb("exps", [P, TOP_K + 1, TILES])
        denom = sb("denom", [P, TILES])
        weight = sb("weight", [P, TOP_K, TILES])
        run_totals = sb("run_totals", [P, N_EXP, TOP_K, TILES + 1])
        run_keep = sb("run_keep", [P, N_EXP, TOP_K, TILES + 1])
        run_before = sb("run_before", [P, N_EXP, TOP_K, TILES + 1])
        ranks = sb("ranks", [P, TOP_K, TILES // BATCH, N_EXP])
        firsts = sb("firsts", [P, TILES // BATCH, N_EXP])
        first_count = sb("first_count", [P, TILES // BATCH])
        rank = sb("rank", [P, TOP_K, TILES])
        kept = sb("kept", [P, TOP_K, TILES])
        slot_base = sb("slot_base", [P, TOP_K, TILES])
        scatter_at = sb("scatter_at", [P, TOP_K, TILES], U32)

        fc_sb = sb("fc_sb", [P, 2, D_HID])
        proj_sb = sb("proj_sb", [P, 2, HT, D_MODEL])
        rows_in = sb("rows_in", [P, 2, SLOT_TILES, ROW])
        tags = sb("tags", [P, N_EXP, SLOT_TILES, 2])
        result_at = sb("result_at", [P, 2, SLOT_TILES], U32)
        result_weight = sb("result_weight", [P, 2, SLOT_TILES])

        x1_chan = x_chan
        hidden = [t[:, :, :].rearrange("p a b -> p (a b)")[:, 0:HT * CAPACITY].rearrange("p (h s) -> p h s", h=HT)
                  for t in (u, dt)]
        rows_chan = product[:, :, :, :].rearrange("p a b c -> p a (b c)")[:, :, 0:CAPACITY]
        rows_out = state[:, :, :, :].rearrange("p a b (j d) -> p a (b j) d", d=D_MODEL)[:, :, 0:SLOT_TILES, :]
        results = dtu[:, :, :].rearrange("p k (j d) -> p (k j) d", d=D_MODEL)

        psum = ctx.enter_context(nc.psum_tensor("psum", [P, 8, CH], F32))
        Y_BANK, A_BANK, B_BANK, C_BANK = 0, 4, 6, 7
        BC_BANK = [B_BANK, C_BANK, B_BANK, Y_BANK + 3]
        DT_BANK = [A_BANK, A_BANK, A_BANK, Y_BANK + 1]

        ident_made = sem("ident_made")
        consts_made = sem("consts_made")
        pads_made = sem("pads_made")
        x_loaded = [sem(f"x_loaded{q}") for q in range(NQ)]
        w_in_loaded = sem("w_in_loaded")
        vectors_loaded = sem("vectors_loaded")
        w_mid_loaded = sem("w_mid_loaded")
        w_late_loaded = sem("w_late_loaded")
        x_turned = sem("x_turned")
        x_chan_ready = sem("x_chan_ready")
        in_projected = sem("in_projected")
        x_in_ready = sem("x_in_ready")
        z_ready = sem("z_ready")
        conv_done = sem("conv_done")
        u_ready = sem("u_ready")
        bc_projected = sem("bc_projected")
        dt_projected = sem("dt_projected")
        bc_taken = sem("bc_taken")
        dt_raw_ready = sem("dt_raw_ready")
        soft_ready = sem("soft_ready")
        soft_step = sem("soft_step")
        dt_ready = sem("dt_ready")
        dtu_ready = sem("dtu_ready")
        last_dtu_ready = sem("last_dtu_ready")
        pick_made = sem("pick_made")
        w_x4_ready = sem("w_x4_ready")
        selector_ready = sem("selector_ready")
        a_ready = sem("a_ready")
        diag_ready = sem("diag_ready")
        dve_step = sem("dve_step")
        act_step = sem("act_step")
        gp_step = sem("gp_step")

        b_spread = sem("b_spread")
        c_spread = sem("c_spread")
        c_ready = sem("c_ready")
        drive_ready = sem("drive_ready")
        decay_ready = sem("decay_ready")
        scanned = sem("scanned")
        product_ready = sem("product_ready")
        summed = sem("summed")
        y_first_ready = sem("y_first_ready")

        gated = sem("gated")
        out_projected = sem("out_projected")
        residual_ready = sem("residual_ready")
        moments_ready = sem("moments_ready")
        rstd_ready = sem("rstd_ready")
        shift_ready = sem("shift_ready")
        x1_ready = sem("x1_ready")
        last_proj_done = sem("last_proj_done")
        last_rows_out_ready = sem("last_rows_out_ready")
        first_added = sem("first_added")
        shift2_ready = sem("shift2_ready")
        late_out_ready = sem("late_out_ready")
        w_g_summed = sem("w_g_summed")
        w_g_sum_copied = sem("w_g_sum_copied")
        x1_turned = sem("x1_turned")
        x1_chan_ready = sem("x1_chan_ready")
        logits_ready = sem("logits_ready")
        above_ready = sem("above_ready")
        exps_ready = sem("exps_ready")
        chosen_ready = sem("chosen_ready")
        ranks_counted = sem("ranks_counted")
        logits_copied = sem("logits_copied")
        ranks_taken = sem("ranks_taken")
        slots_ready = sem("slots_ready")
        blanks_made = sem("blanks_made")
        rows_cleared = sem("rows_cleared")
        scattered = sem("scattered")
        early_scattered = sem("early_scattered")
        fc_loaded = [sem(f"fc_loaded{i}") for i in range(2)]
        proj_loaded = [sem(f"proj_loaded{i}") for i in range(2)]
        rows_loaded = [sem(f"rows_loaded{i}") for i in range(2)]
        rows_turned = sem("rows_turned")
        rows_chan_ready = sem("rows_chan_ready")
        fc_done = sem("fc_done")
        hidden_ready = sem("hidden_ready")
        proj_done = sem("proj_done")
        rows_out_ready = sem("rows_out_ready")
        tags_copied = sem("tags_copied")
        result_tagged = sem("result_tagged")
        results_sent = [sem(f"results_sent{i}") for i in range(2)]
        results_loaded = [[sem(f"results{k}_loaded{g}") for g in range(NQ)] for k in range(TOP_K)]
        sent_copied = sem("sent_copied")
        sent_tagged = sem("sent_tagged")
        moments2_ready = sem("moments2_ready")
        rstd2_ready = sem("rstd2_ready")
        out_ready = sem("out_ready")
        out_stored = sem("out_stored")

        block = ctx.enter_context(nc.Block())
        x_rows = x.rearrange("b (j p) d -> p (b j) d", p=P)
        out_rows = out.rearrange("b (j p) d -> p (b j) d", p=P)
        LAST = BATCH * D_STATE - 1
        LAST_BANKS = [[0, 1, 6, 7, 2], [3, 4, 5, 0, 1]]
        GROUPS = TILES // TPC
        HALF_TILES = TILES // BATCH
        COUNTS = TOP_K * HALF_TILES * N_EXP

        @block.sync
        def _(sp):
            for q in range(NQ):
                sp.dma_start(x_tok[:, TPC * q:TPC * (q + 1), :], x_rows[:, TPC * q:TPC * (q + 1), :]).then_inc(x_loaded[q], 16)
                if q == 0:
                    sp.dma_start(w_in_sb[:, :], W_in).then_inc(w_in_loaded, 16)
            sp.dma_start(w_out_sb[:, :, :], W_out.rearrange("(t p) m -> p t m", p=P)).then_inc(w_late_loaded, 16)
            sp.dma_start(w_g_sb[:, :], w_g).then_inc(w_late_loaded, 16)
            sp.wait_ge(blanks_made, 2)
            blank_slots = slot_rows.rearrange("(g p r) d -> g p (r d)", g=CLEARS, p=P)
            blank_results = result_rows.rearrange("(g p r) d -> g p (r d)", g=CLEARS, p=P)
            for g in range(CLEARS):
                sp.dma_start(blank_slots[g], blank[:, :, :].rearrange("p r d -> p (r d)")).then_inc(rows_cleared, 16)
                sp.dma_start(blank_results[g], zeros[:, :]).then_inc(rows_cleared, 16)

            def load_first(g, i):
                sp.dma_start(fc_sb[:, i, :], c_fc[bass.ds(2 * g + i, 1), :, :].rearrange("e p m -> p (e m)")).then_inc(fc_loaded[i], 16)

            def load_second(g, i):
                sp.dma_start(proj_sb[:, i, :, :],
                             c_proj[bass.ds(2 * g + i, 1), :, :].rearrange("e (h p) m -> p (e h) m", p=P)).then_inc(proj_loaded[i], 16)

            def load_rows(g, i):
                sp.dma_start(rows_in[:, i, :, :],
                             slot_rows[bass.ds((2 * g + i) * CAPACITY, CAPACITY), :].rearrange("(s p) d -> p s d", p=P)).then_inc(rows_loaded[i], 16)

            for i in range(2):
                load_first(0, i)
                load_second(0, i)
            sp.wait_ge(early_scattered, 16 * HALF_TILES)
            sp.wait_ge(scattered, 16 * (RUNS - HALF_TILES))
            for i in range(2):
                load_rows(0, i)
            with sp.Fori(1, PAIRS) as g:
                for i in range(2):
                    e = 2 * g + i
                    sp.wait_ge(rows_turned, e - 1)
                    sp.wait_ge(tags_copied, e - 1)
                    load_rows(g, i)
                    sp.wait_ge(fc_done, HT * (e - 1))
                    load_first(g, i)
                    sp.wait_ge(proj_done, e - 1)
                    load_second(g, i)

            for i in range(2):
                sp.wait_ge(results_sent[i], 16 * SLOT_TILES * PAIRS)
            in_order = result_rows.rearrange("(k j p) d -> p (k j) d", k=TOP_K, p=P)
            for g, k in ((0, 0), (1, 0), (0, 1), (2, 0), (1, 1), (3, 0), (2, 1), (3, 1)):
                at = slice(k * TILES + TPC * g, k * TILES + TPC * (g + 1))
                sp.dma_start(results[:, at, :], in_order[:, at, :]).then_inc(results_loaded[k][g], 16)

            for g in range(GROUPS):
                if g < NCH:
                    sp.wait_ge(out_ready, TPC * (g + 1))
                else:
                    sp.wait_ge(out_ready, TPC * NCH + TPC // 2 * (g - NCH + 1))
                    sp.wait_ge(late_out_ready, TPC // 2 * (g - NCH + 1))
                sp.dma_start(out_rows[:, TPC * g:TPC * (g + 1), :], final[:, TPC * g:TPC * (g + 1), :]).then_inc(out_stored, 16)
            sp.wait_ge(out_stored, 16 * GROUPS)

        @block.tensor
        def _(pe):
            pe.wait_ge(ident_made, 2)

            def turn_x(q):
                pe.wait_ge(x_loaded[q], 16)
                if q:
                    pe.wait_ge(x_chan_ready, q)
                for j in range(TPC):
                    last = nc.tensor.transpose(psum[:, C_BANK, j * P:(j + 1) * P], x_tok[:, TPC * q + j, :], ident[:, :])
                last.then_inc(x_turned, 1)

            def project_in(q):
                pe.wait_ge(x_chan_ready, q + 1)
                for r in range(2 * DT):
                    if q and r < DT:
                        pe.wait_ge(x_in_ready, DT * (q - 1) + r + 1)
                    elif q:
                        pe.wait_ge(z_ready, DT * (q - 1) + r - DT + 1)
                    nc.tensor.matmul(psum[:, Y_BANK + r, :], w_in_sb[:, r * P:(r + 1) * P], x_chan[:, q * CH:(q + 1) * CH],
                                     start=True, stop=True).then_inc(in_projected, 1)

            def project_bc(q):
                for k in range(DT):
                    last = nc.tensor.matmul(psum[:, BC_BANK[q], :], w_x4[:, k, :, :].rearrange("p a b -> p (a b)"),
                                            u[:, k, q * CH:(q + 1) * CH], start=(k == 0), stop=(k == DT - 1))
                last.then_inc(bc_projected, 1)

            def project_dt(q, r):
                for k in range(DT):
                    last = nc.tensor.matmul(psum[:, DT_BANK[q] + r, :], w_dt_sb[:, k, r * P:(r + 1) * P],
                                            u[:, k, q * CH:(q + 1) * CH], start=(k == 0), stop=(k == DT - 1))
                last.then_inc(dt_projected, 1)

            for _ in range(10):
                nc.tensor.transpose(psum[:, Y_BANK, 0:P], ident[:, :], ident[:, :])
            turn_x(0)
            pe.wait_ge(w_in_loaded, 16)
            for q in range(NQ):
                if q + 1 < NQ:
                    turn_x(q + 1)
                project_in(q)
                if q == 1:
                    pe.wait_ge(w_x4_ready, 1)
                    pe.wait_ge(u_ready, DT)
                    project_bc(0)
                    for r in range(DT):
                        project_dt(0, r)
            pe.wait_ge(u_ready, DT * 2)
            pe.wait_ge(x_chan_ready, NQ)
            project_bc(1)
            for r in range(DT):
                pe.wait_ge(dt_raw_ready, r + 1)
                project_dt(1, r)
            pe.wait_ge(u_ready, DT * 3)
            pe.wait_ge(bc_taken, 1)
            project_bc(2)
            for r in range(DT):
                pe.wait_ge(dt_raw_ready, DT + r + 1)
                project_dt(2, r)

            def spread_b(i, b, c):
                n = i - D_STATE * b
                first = isinstance(i, int) and i == 0
                parts = bc_parts[:, b * SEQ + c * CH:b * SEQ + (c + 1) * CH]
                if not (first and c == 0):
                    pe.wait_ge(drive_ready, UNITS * i + DT * c)
                nc.tensor.matmul(psum[:, B_BANK, :], selector[:, bass.ds(n, 1), :].rearrange("p a b -> p (a b)"), parts,
                                 start=True, stop=True).then_inc(b_spread, 1)

            def spread_c(i, b, c):
                n = i - D_STATE * b
                first = isinstance(i, int) and i == 0
                parts = bc_parts[:, b * SEQ + c * CH:b * SEQ + (c + 1) * CH]
                if not (first and c == 0):
                    pe.wait_ge(c_ready, NCH * i + c)
                nc.tensor.matmul(psum[:, C_BANK, :], selector[:, bass.ds(n + D_STATE, 1), :].rearrange("p a b -> p (a b)"), parts,
                                 start=True, stop=True).then_inc(c_spread, 1)

            def add_to_y(i, c):
                for d in range(DT):
                    pe.wait_ge(product_ready, UNITS * i + DT * c + d + 1)
                    nc.tensor.matmul(psum[:, Y_BANK + DT * c + d, :], ident[:, :], product[:, c, d, :],
                                     start=False, stop=True, skip_group_check=True).then_inc(summed, 1)

            def start_y(b, c, channels=range(DT)):
                for d in channels:
                    t = b * SEQ + c * CH
                    nc.tensor.matmul(psum[:, Y_BANK + DT * c + d, :], diag_d[:, d, :], u[:, d, t:t + CH],
                                     start=True, stop=True, skip_group_check=True)

            def states(i, b):
                spread_b(i, b, 0)
                add_to_y(i - 2, 1)
                spread_c(i, b, 0)
                spread_b(i, b, 1)
                add_to_y(i - 1, 0)
                spread_c(i, b, 1)

            pe.wait_ge(selector_ready, 1)
            pe.wait_ge(bc_taken, 2)
            spread_c(0, 0, 0)
            pe.wait_ge(u_ready, DT * NQ)
            pe.wait_ge(z_ready, DT * NQ)
            pe.wait_ge(x_in_ready, DT * NQ)
            project_bc(3)
            project_dt(3, 0)
            pe.wait_ge(bc_taken, 3)
            spread_b(0, 0, 0)
            project_dt(3, 1)
            pe.wait_ge(diag_ready, DT)
            start_y(0, 0, [0])
            spread_b(0, 0, 1)
            pe.wait_ge(dt_raw_ready, DT * NQ - 1)
            start_y(0, 0, [1])
            spread_c(0, 0, 1)
            spread_b(1, 0, 0)
            pe.wait_ge(dt_raw_ready, DT * NQ)
            start_y(0, 1, [0])
            spread_c(1, 0, 0)
            spread_b(1, 0, 1)
            pe.wait_ge(bc_taken, NQ)
            start_y(0, 1, [1])
            add_to_y(0, 0)
            spread_c(1, 0, 1)
            with pe.Fori(2, D_STATE) as i:
                states(i, 0)
            states(D_STATE, 1)
            spread_b(D_STATE + 1, 1, 0)
            add_to_y(D_STATE - 1, 1)
            spread_c(D_STATE + 1, 1, 0)
            spread_b(D_STATE + 1, 1, 1)
            for c in range(NCH):
                pe.wait_ge(y_first_ready, DT * (c + 1))
                start_y(1, c)
            add_to_y(D_STATE, 0)
            spread_c(D_STATE + 1, 1, 1)
            with pe.Fori(D_STATE + 2, 2 * D_STATE) as i:
                states(i, 1)
            add_to_y(LAST - 1, 1)

            OUT_BANKS = [B_BANK, C_BANK, Y_BANK, Y_BANK + 1]
            pe.wait_ge(w_late_loaded, 32)

            def project_out(g):
                pe.wait_ge(gated, DT * (g + 1))
                for j in range(TPC):
                    for k in range(DT):
                        t = (TPC * g + j) * P
                        last = nc.tensor.matmul(psum[:, OUT_BANKS[g], j * P:(j + 1) * P], z_gate[:, k, t:t + P], w_out_sb[:, k, :],
                                                start=(k == 0), stop=(k == DT - 1))
                last.then_inc(out_projected, 1)

            def turn_x1(g):
                pe.wait_ge(residual_ready, g + 1)
                if g >= 2:
                    pe.wait_ge(x1_chan_ready, g - 1)
                for j in range(TPC):
                    last = nc.tensor.transpose(psum[:, A_BANK + g % 2, j * P:(j + 1) * P], x1[:, TPC * g + j, :], ident[:, :])
                last.then_inc(x1_turned, 1)

            def make_logits(b):
                for g in range(NCH * b, NCH * (b + 1)):
                    pe.wait_ge(x1_chan_ready, g + 1)
                    for j in range(TPC * g, TPC * (g + 1)):
                        last = nc.tensor.matmul(psum[:, B_BANK, j * N_EXP:(j + 1) * N_EXP], x1_chan[:, j * P:(j + 1) * P], w_g_sb[:, :],
                                                start=True, stop=True)
                last.then_inc(logits_ready, 1)

            def count_choices(b):
                marks = chosen[:, b, :, :, :].rearrange("p k j e -> p (k j e)")
                at = slice(b * COUNTS, (b + 1) * COUNTS)
                totals_at = slice((BATCH + b) * COUNTS, (BATCH + b + 1) * COUNTS)
                pe.wait_ge(chosen_ready, b + 1)
                nc.tensor.matmul(psum[:, C_BANK, at], upto[:, :], marks, start=True, stop=True)
                nc.tensor.matmul(psum[:, C_BANK, totals_at], ones[:, :], marks, start=True, stop=True).then_inc(ranks_counted, 1)

            pe.wait_ge(drive_ready, UNITS * (LAST + 1))
            project_out(0)
            pe.wait_ge(c_ready, NCH * (LAST + 1))
            project_out(1)
            pe.wait_ge(scanned, UNITS * (LAST + 1))
            turn_x1(0)
            add_to_y(LAST, 0)
            turn_x1(1)
            nc.tensor.matmul(psum[:, C_BANK, 0:N_EXP], ones_wide[:, :], w_g_sb[:, :], start=True, stop=True).then_inc(w_g_summed, 1)
            make_logits(0)
            add_to_y(LAST, 1)
            project_out(2)
            pe.wait_ge(w_g_sum_copied, 1)
            count_choices(0)
            project_out(3)
            turn_x1(2)
            turn_x1(3)
            pe.wait_ge(logits_copied, 1)
            make_logits(1)
            pe.wait_ge(ranks_taken, 1)
            count_choices(1)

            def turn_rows(g, i):
                e = 2 * g + i
                pe.wait_ge(rows_loaded[i], 16 * (g + 1))
                if not (isinstance(e, int) and e == 0):
                    pe.wait_ge(rows_chan_ready, e)
                for s in range(SLOT_TILES):
                    last = nc.tensor.transpose(psum[:, s // TPC, (s % TPC) * P:(s % TPC + 1) * P], rows_in[:, i, s, 0:D_MODEL], ident[:, :])
                last.then_inc(rows_turned, 1)

            def first_layer(g, i):
                e = 2 * g + i
                first = isinstance(e, int) and e == 0
                pe.wait_ge(fc_loaded[i], 16 * (g + 1))
                pe.wait_ge(rows_chan_ready, e + 1)
                for h in range(HT):
                    if not (first and h < 2):
                        pe.wait_ge(hidden_ready, HT * e + h - 1)
                    for s in range(2):
                        last = nc.tensor.matmul(psum[:, 2 + 2 * (h % 2) + s, 0:HALF], fc_sb[:, i, h * P:(h + 1) * P],
                                                rows_chan[:, i, s * HALF:(s + 1) * HALF], start=True, stop=True)
                    last.then_inc(fc_done, 1)

            def second_layer(g, i):
                e = 2 * g + i
                pe.wait_ge(proj_loaded[i], 16 * (g + 1))
                pe.wait_ge(hidden_ready, HT * (e + 1))
                last_pair = isinstance(g, int) and g == PAIRS - 1
                if not (last_pair and i == 1 or isinstance(e, int) and e == 0):
                    pe.wait_ge(rows_out_ready, e)
                if last_pair:
                    pe.wait_ge(hidden_ready, HT * N_EXP)
                for s in range(SLOT_TILES):
                    bank, at = (LAST_BANKS[i][s], 0) if last_pair else (6 + s // TPC, s % TPC)
                    if last_pair and i == 1 and bank < 2:
                        pe.wait_ge(last_rows_out_ready, bank + 1)
                    for h in range(HT):
                        last = nc.tensor.matmul(psum[:, bank, at * P:(at + 1) * P], hidden[i][:, h, s * P:(s + 1) * P],
                                                proj_sb[:, i, h, :], start=(h == 0), stop=(h == HT - 1))
                    if last_pair:
                        last.then_inc(last_proj_done, 1)
                if not last_pair:
                    last.then_inc(proj_done, 1)

            pe.wait_ge(ranks_taken, 2)
            pe.wait_ge(scattered, 16 * (RUNS - HALF_TILES))
            for _ in range(20):
                nc.tensor.transpose(psum[:, 2, 0:P], ident[:, :], ident[:, :])
            turn_rows(0, 0)
            first_layer(0, 0)
            turn_rows(0, 1)

            def expert_pair(g):
                first_layer(g, 1)
                turn_rows(g + 1, 0)
                second_layer(g, 0)
                first_layer(g + 1, 0)
                turn_rows(g + 1, 1)
                second_layer(g, 1)

            expert_pair(0)
            with pe.Fori(1, PAIRS - 1) as g:
                expert_pair(g)
            first_layer(PAIRS - 1, 1)
            second_layer(PAIRS - 1, 0)
            second_layer(PAIRS - 1, 1)

        @block.scalar
        def _(act):
            step = Tally()
            act.dma_start(channel_sb[:, :, :], channel_values).then_inc(vectors_loaded, 16)
            act.dma_start(a_log_sb[:, :], A_log.partition_broadcast(P)).then_inc(vectors_loaded, 16)
            act.dma_start(w_x_sb[:, :, :], W_x.rearrange("(t p) m -> p t m", p=P)).then_inc(w_mid_loaded, 16)
            act.dma_start(w_dt_sb[:, :, :], W_dt.rearrange("(t p) m -> p t m", p=P)).then_inc(w_mid_loaded, 16)

            def activate_u(q):
                for d in range(DT):
                    act.wait_ge(conv_done, DT * q + d + 1)
                    part = u[:, d, q * CH:(q + 1) * CH]
                    nc.scalar.activation(part, part, ACT.Silu).then_inc(u_ready, 1)

            def add_dt_bias(q):
                for d in range(DT):
                    act.wait_ge(dt_projected, DT * q + d + 1)
                    nc.scalar.activation(dt[:, d, q * CH:(q + 1) * CH], psum[:, DT_BANK[q] + d, :], ACT.Identity,
                                         bias=b_dt_sb[:, d:d + 1]).then_inc(dt_raw_ready, 1)

            act.preload_act_table(ACT.Silu)
            act.wait_ge(pick_made, 1)
            nc.scalar.activation(selector[:, :, :], pick[:, :].unsqueeze(2).to_broadcast([P, 2 * D_STATE, P]),
                                 ACT.Copy).then_inc(selector_ready, 1)

            def copy_x_in(q):
                b, c = divmod(q, NCH)
                for d in range(DT):
                    act.wait_ge(in_projected, 2 * DT * q + d + 1)
                    nc.scalar.activation(x_in[:, d, b, PAD + c * CH:PAD + (c + 1) * CH], psum[:, Y_BANK + d, :],
                                         ACT.Copy).then_inc(x_in_ready, 1)

            def activate_z(q):
                for d in range(DT):
                    act.wait_ge(in_projected, 2 * DT * q + DT + d + 1)
                    nc.scalar.activation(z_gate[:, d, q * CH:(q + 1) * CH], psum[:, Y_BANK + DT + d, :],
                                         ACT.Silu).then_inc(z_ready, 1)

            copy_x_in(0)
            activate_z(0)
            copy_x_in(1)
            act.wait_ge(vectors_loaded, 16 * 2)
            activate_u(0)
            activate_z(1)
            add_dt_bias(0)
            copy_x_in(2)
            activate_u(1)
            activate_z(2)
            copy_x_in(3)
            activate_z(3)
            activate_u(2)
            add_dt_bias(1)
            activate_u(3)

            act.preload_act_table_set("natural_log_exp_and_others")
            nc.scalar.activation(a_exp[:, :], a_log_sb[:, :], ACT.Exp).then_inc(act_step, 1)
            act.wait_ge(act_step, step.up())
            for k in range(UNITS):
                nc.scalar.mul(a_neg[:, k, :], a_exp[:, :], -1.0).then_inc(a_ready, 1)

            def softplus(q):
                for d in range(DT):
                    k = DT * q + d
                    act.wait_ge(dt_raw_ready, k + 1)
                    if k >= 2 * DT:
                        act.wait_ge(dt_ready, k - 2 * DT + 1)
                    nc.scalar.activation(soft[:, q % 2, d, :], dt[:, d, q * CH:(q + 1) * CH], ACT.Abs).then_inc(act_step, 1)
                    step.up()
                first = step.n - DT
                for func, args in ((ACT.Exp, {"scale": -1.0}), (ACT.Ln, {"bias": 1.0})):
                    for d in range(DT):
                        act.wait_ge(act_step, first + d + 1)
                        done = act_step if func == ACT.Exp else soft_ready
                        nc.scalar.activation(soft[:, q % 2, d, :], soft[:, q % 2, d, :], func, **args).then_inc(done, 1)
                    if func == ACT.Exp:
                        first = step.n
                        step.up(DT)

            def soften(q, d, func):
                part = soft[:, q % 2, d, :]
                if func == ACT.Abs:
                    act.wait_ge(dt_raw_ready, DT * q + d + 1)
                    act.wait_ge(dt_ready, DT * (q - 2) + d + 1)
                    nc.scalar.activation(part, dt[:, d, q * CH:(q + 1) * CH], func).then_inc(act_step, 1)
                    step.up()
                elif func == ACT.Exp:
                    act.wait_ge(act_step, step.n)
                    nc.scalar.activation(part, part, func, scale=-1.0).then_inc(act_step, 1)
                    step.up()
                else:
                    act.wait_ge(act_step, step.n)
                    nc.scalar.activation(part, part, func, bias=1.0).then_inc(soft_ready, 1)

            softplus(0)
            add_dt_bias(2)
            softplus(1)

            act.wait_ge(a_ready, UNITS)
            assert (NQ, DT) == (4, 2)
            act.wait_ge(dt_raw_ready, DT * (NQ - 1))

            def decays(i, b, chunks=range(NCH)):
                n = i - D_STATE * b
                first = isinstance(i, int) and i == 0
                for c in chunks:
                    if first:
                        act.wait_ge(dt_ready, DT * (c + 1))
                    for d in range(DT):
                        if not (first and c == 0):
                            act.wait_ge(scanned, UNITS * i + DT * c + d - 1)
                        t = b * SEQ + c * CH
                        nc.scalar.activation(psum[:, A_BANK + d, :], dt[:, d, t:t + CH], ACT.Exp,
                                             scale=a_neg[:, DT * c + d, bass.ds(n, 1)]).then_inc(decay_ready, 1)
                    act.wait_ge(c_spread, NCH * i + c + 1)
                    if not first:
                        act.wait_ge(product_ready, UNITS * (i - 1) + DT * (c + 1))
                    nc.scalar.activation(c_wide[:, c, :], psum[:, C_BANK, :], ACT.Copy).then_inc(c_ready, 1)

            for i, (q, d) in enumerate(((2, 0), (2, 1), (3, 0), (3, 1))):
                decays(i, 0, [0])
                if i == 0:
                    add_dt_bias(3)
                soften(q, d, ACT.Abs)
                decays(i, 0, [1])
                soften(q, d, ACT.Exp)
                soften(q, d, ACT.Ln)
            with act.Fori(4, D_STATE) as i:
                decays(i, 0)
            act.wait_ge(dt_ready, DT * NQ)
            decays(D_STATE, 1)
            for c in range(NCH):
                for d in range(DT):
                    act.wait_ge(summed, UNITS * (D_STATE - 1) + DT * c + d + 1)
                    nc.scalar.activation(y_first[:, c, d, :], psum[:, Y_BANK + DT * c + d, :], ACT.Copy).then_inc(y_first_ready, 1)
                decays(D_STATE + 1, 1, [c])
            with act.Fori(D_STATE + 2, 2 * D_STATE) as i:
                decays(i, 1)

            def inverse_root(tiles, ready, value, done):
                act.wait_ge(ready, value)
                nc.scalar.activation(log_var[:, tiles], moments[:, tiles, 1], ACT.Ln, scale=-2.0).then_inc(act_step, 1)
                act.wait_ge(act_step, step.up())
                nc.scalar.activation(rstd[:, tiles], log_var[:, tiles], ACT.Exp, scale=-0.5).then_inc(done, 1)

            def normalize(rows, g, done, count=TPC):
                for j in range(TPC * g, TPC * g + count):
                    nc.scalar.activation(rows[:, j, :], rows[:, j, :], ACT.Identity, scale=rstd[:, j:j + 1],
                                         bias=shift[:, j:j + 1]).then_inc(done, 1)

            for b in range(BATCH):
                half = slice(HALF_TILES * b, HALF_TILES * (b + 1))
                for g in range(NCH * b, NCH * (b + 1)):
                    act.wait_ge(x1_turned, g + 1)
                    nc.scalar.activation(x1_chan[:, g * CH:(g + 1) * CH], psum[:, A_BANK + g % 2, :], ACT.Copy).then_inc(x1_chan_ready, 1)
                inverse_root(half, moments_ready, b + 1, rstd_ready)
                act.wait_ge(shift_ready, b + 1)
                for g in range(NCH * b, NCH * (b + 1)):
                    normalize(x1, g, x1_ready)
                act.wait_ge(above_ready, 2 * (b + 1))
                nc.scalar.activation(exps[:, :, half], above[:, :, half], ACT.Exp).then_inc(exps_ready, 1)
                for g in range(NCH * b, NCH * (b + 1)):
                    act.wait_ge(x1_ready, TPC * (g + 1))
                    tiles = slice(TPC * g, TPC * (g + 1))
                    nc.scalar.activation(sent[:, 1, tiles, 0:D_MODEL], sent[:, 0, tiles, 0:D_MODEL], ACT.Copy).then_inc(sent_copied, 1)

            act.preload_act_table(ACT.Gelu)

            def activate_hidden(g, i):
                e = 2 * g + i
                first = isinstance(g, int) and g == 0
                if not first:
                    act.wait_ge(proj_done, e - 1)
                for h in range(HT):
                    act.wait_ge(fc_done, HT * e + h + 1)
                    nc.scalar.activation(hidden[i][:, h, :].rearrange("p (s k) -> p s k", s=2),
                                         psum[:, 2 + 2 * (h % 2):4 + 2 * (h % 2), 0:HALF], ACT.Gelu).then_inc(hidden_ready, 1)

            for i in range(2):
                activate_hidden(0, i)
            with act.Fori(1, PAIRS) as g:
                for i in range(2):
                    activate_hidden(g, i)

            act.preload_act_table_set("natural_log_exp_and_others")
            for g in range(GROUPS):
                inverse_root(slice(TPC * g, TPC * (g + 1)), moments2_ready, g + 1, rstd2_ready)
                if g:
                    act.wait_ge(shift2_ready, g)
                    normalize(final, g - 1, out_ready, TPC if g - 1 < NCH else TPC // 2)
            act.wait_ge(shift2_ready, GROUPS)
            normalize(final, GROUPS - 1, out_ready, TPC // 2)

        @block.gpsimd
        def _(gp):
            step = Tally()
            nc.gpsimd.memset(ident[:, :], 0.0).then_inc(ident_made, 1)
            gp.wait_ge(ident_made, 1)
            nc.gpsimd.affine_select(out=ident[:, :], in_=ident[:, :], compare_op=ALU.not_equal, fill=1.0, base=0,
                                    pattern=[[-1, P]], channel_multiplier=1).then_inc(ident_made, 1)
            nc.gpsimd.memset(pick[:, :], 0.0).then_inc(gp_step, 1)
            for base in (0, 64, 96):
                gp.wait_ge(gp_step, step.up())
                nc.gpsimd.affine_select(out=pick[:, :], in_=pick[:, :], compare_op=ALU.not_equal, fill=1.0, base=-base,
                                        pattern=[[-1, 2 * D_STATE]], channel_multiplier=1).then_inc(pick_made if base == 96 else gp_step, 1)
            nc.gpsimd.memset(upto[:, :], 1.0).then_inc(gp_step, 1)
            gp.wait_ge(gp_step, step.up())
            nc.gpsimd.affine_select(out=upto[:, :], in_=upto[:, :], compare_op=ALU.is_ge, fill=0.0, base=0,
                                    pattern=[[1, P]], channel_multiplier=-1).then_inc(gp_step, 1)
            nc.gpsimd.memset(ones[:, :], 1.0).then_inc(gp_step, 1)
            nc.gpsimd.memset(ones_wide[:, :], 1.0).then_inc(gp_step, 1)
            nc.gpsimd.iota(expert_number[:, :], pattern=[[1, N_EXP]], base=0, channel_multiplier=0,
                           allow_small_or_imprecise_dtypes=True).then_inc(gp_step, 1)
            nc.gpsimd.memset(run_totals[:, :, :, :], 0.0).then_inc(gp_step, 1)
            nc.gpsimd.memset(run_keep[:, :, :, :], 1.0).then_inc(gp_step, 1)
            gp.wait_ge(gp_step, step.up(6))
            nc.gpsimd.memset(run_keep[:, :, :, 0:1], 0.0).then_inc(consts_made, 1)
            nc.gpsimd.memset(blank[:, :, :], 0.0).then_inc(gp_step, 1)
            gp.wait_ge(gp_step, step.up())
            nc.gpsimd.memset(blank[:, :, ROW_TO:ROW_TO + 1], float(NOWHERE)).then_inc(blanks_made, 1)
            nc.gpsimd.memset(zeros[:, :], 0.0).then_inc(blanks_made, 1)
            nc.gpsimd.iota(sent[:, :, :, ROW_TO], pattern=[[TOKENS, TOP_K], [P, TILES]], base=0, channel_multiplier=1,
                           allow_small_or_imprecise_dtypes=True).then_inc(sent_tagged, 1)
            gp.wait_ge(vectors_loaded, 16 * 2)
            for d in range(DT):
                nc.gpsimd.tensor_tensor(diag_d[:, d, :], ident[:, :], d_sb[:, d:d + 1].to_broadcast([P, P]), ALU.mult).then_inc(diag_ready, 1)

            def times_u(q):
                for d in range(DT):
                    gp.wait_ge(dt_ready, DT * q + d + 1)
                    at = slice(q * CH, (q + 1) * CH)
                    nc.gpsimd.tensor_tensor(dtu[:, d, at], dt[:, d, at], u[:, d, at], ALU.mult).then_inc(dtu_ready, 1)

            for q in range(NCH):
                times_u(q)

            def products(i, states=state):
                first = isinstance(i, int) and i == 0
                for c in range(NCH):
                    gp.wait_ge(c_ready, NCH * i + c + 1)
                    gp.wait_ge(scanned, UNITS * i + DT * (c + 1))
                    if not first:
                        gp.wait_ge(summed, UNITS * (i - 1) + DT * (c + 1))
                    nc.gpsimd.tensor_tensor(product[:, c, :, :], states[:, c, :, :],
                                            c_wide[:, c, :].unsqueeze(1).to_broadcast([P, DT, CH]), ALU.mult).then_inc(product_ready, DT)

            products(0)
            for i in range(1, 4):
                products(i)
            times_u(NCH)
            with gp.Fori(2, BATCH * D_STATE // 2) as g:
                products(2 * g, soft)
                products(2 * g + 1, state)

            gp.wait_ge(rows_cleared, 16 * 2 * CLEARS)
            gp.wait_ge(sent_tagged, 1)

            def scatter(k, j, done=scattered):
                gp.indirect_dma_start(out=slot_rows, out_offset=bass.IndirectOffsetOnAxis(ap=scatter_at[:, k, j:j + 1], axis=0),
                                      in_=sent[:, k, j, :], in_offset=None, bounds_check=SLOTS - 1,
                                      oob_is_err=False).then_inc(done, 16)

            gp.wait_ge(slots_ready, 2)
            gp.wait_ge(x1_ready, HALF_TILES)
            gp.wait_ge(sent_copied, NCH)
            for j in range(HALF_TILES):
                scatter(1, j, early_scattered)
            for j in range(HALF_TILES):
                scatter(0, j)
            gp.wait_ge(slots_ready, 4)
            gp.wait_ge(x1_ready, TILES)
            gp.wait_ge(sent_copied, GROUPS)
            gp.wait_ge(early_scattered, 16 * HALF_TILES)
            for k in range(TOP_K):
                for j in range(HALF_TILES, TILES):
                    scatter(k, j)
            for g in range(PAIRS):
                for i in range(2):
                    last_pair = g == PAIRS - 1
                    if not last_pair:
                        gp.wait_ge(rows_out_ready, 2 * g + i + 1)
                    for s in range(SLOT_TILES):
                        if last_pair:
                            gp.wait_ge(last_rows_out_ready, SLOT_TILES * i + s + 1)
                        gp.indirect_dma_start(out=result_rows, out_offset=bass.IndirectOffsetOnAxis(ap=result_at[:, i, s:s + 1], axis=0),
                                              in_=rows_out[:, i, s, :], in_offset=None, bounds_check=RESULTS - 1,
                                              oob_is_err=False).then_inc(results_sent[i], 16)

            gp.wait_ge(x1_ready, TILES)
            for g in range(GROUPS):
                tiles = slice(TPC * g, TPC * (g + 1))
                gp.wait_ge(results_loaded[0][g], 16)
                nc.gpsimd.tensor_tensor(final[:, tiles, :], x1[:, tiles, :], results[:, tiles, :], ALU.add).then_inc(first_added, 1)

        @block.vector
        def _(dve):
            step = Tally()
            for b in range(BATCH):
                nc.vector.memset(x_in[:, :, b, 0:PAD], 0.0).then_inc(pads_made, 1)

            def copy_x(q):
                dve.wait_ge(x_turned, q + 1)
                nc.vector.tensor_copy(x_chan[:, q * CH:(q + 1) * CH], psum[:, C_BANK, :]).then_inc(x_chan_ready, 1)

            def convolve(q):
                b, c = divmod(q, NCH)
                for d in range(DT):
                    dve.wait_ge(x_in_ready, DT * q + d + 1)
                    nc.vector.tensor_scalar(u[:, d, q * CH:(q + 1) * CH], x_in[:, d, b, c * CH:(c + 1) * CH],
                                            conv_w_sb[:, d, 0:1], conv_b_sb[:, d:d + 1], ALU.mult, ALU.add).then_inc(dve_step, 1)
                for k in range(1, D_CONV):
                    first = step.up(DT) - DT
                    for d in range(DT):
                        dve.wait_ge(dve_step, first + d + 1)
                        part = u[:, d, q * CH:(q + 1) * CH]
                        nc.vector.scalar_tensor_tensor(part, x_in[:, d, b, c * CH + k:(c + 1) * CH + k], conv_w_sb[:, d, k:k + 1], part,
                                                       ALU.mult, ALU.add).then_inc(conv_done if k == PAD else dve_step, 1)

            def take_scan_inputs(q):
                at = slice(q * CH, (q + 1) * CH)
                dve.wait_ge(bc_projected, q + 1)
                nc.vector.tensor_copy(bc_parts[:, at], psum[:, BC_BANK[q], :]).then_inc(dve_step, 1)
                high_done = step.up()
                dve.wait_ge(dve_step, high_done)
                nc.vector.tensor_tensor(bc_rest[64:, :], psum[64:, BC_BANK[q], :], bc_parts[64:, at], ALU.subtract).then_inc(dve_step, 1)
                rest_done = step.up()
                dve.wait_ge(dve_step, rest_done)
                nc.vector.tensor_copy(bc_parts[64:, at], bc_rest[64:, :]).then_inc(dve_step, 1)
                dve.wait_ge(dve_step, step.up())
                nc.vector.tensor_tensor(bc_parts[96:, at], bc_rest[96:, :], bc_parts[96:, at], ALU.subtract).then_inc(bc_taken, 1)

            copy_x(0)
            dve.wait_ge(vectors_loaded, 16 * 2)
            dve.wait_ge(pads_made, BATCH)
            for q in range(NQ):
                if q + 1 < NQ:
                    copy_x(q + 1)
                convolve(q)
                if q == 1:
                    take_scan_inputs(0)
                if q == 0:
                    dve.wait_ge(w_mid_loaded, 32)
                    nc.vector.tensor_copy(w_x4[:, :, :, :], w_x_sb[:, :, :].unsqueeze(2).to_broadcast([P, DT, 4, 2 * D_STATE])).then_inc(w_x4_ready, 1)
            take_scan_inputs(1)
            take_scan_inputs(2)

            def finish_dt(q, d):
                dve.wait_ge(soft_ready, DT * q + d + 1)
                part = dt[:, d, q * CH:(q + 1) * CH]
                nc.vector.scalar_tensor_tensor(part, part, 0.0, soft[:, q % 2, d, :], ALU.max, ALU.add).then_inc(dt_ready, 1)

            for d in range(DT):
                finish_dt(0, d)
            take_scan_inputs(3)

            def drives(i, b, c):
                t = b * SEQ + c * CH
                if isinstance(i, int) and i == 0:
                    dve.wait_ge(dtu_ready, DT * (c + 1))
                dve.wait_ge(b_spread, NCH * i + c + 1)
                if not (isinstance(i, int) and i == 0):
                    dve.wait_ge(scanned, UNITS * (i - 1) + DT * (c + 1))
                nc.vector.tensor_tensor(drive[:, c, :, :], dtu[:, :, t:t + CH],
                                        psum[:, B_BANK, :].unsqueeze(1).to_broadcast([P, DT, CH]), ALU.mult).then_inc(drive_ready, DT)

            def scan_channels(i, c, d, states, reused):
                unit = UNITS * i + DT * c + d
                dve.wait_ge(decay_ready, unit + 1)
                dve.wait_ge(drive_ready, unit + 1)
                if not (isinstance(i, int) and i == 0):
                    dve.wait_ge(product_ready, unit - UNITS * reused + 1)
                if c:
                    dve.wait_ge(scanned, unit - DT + 1)
                before = states[:, c - 1, d, CH - 1:CH] if c else 0.0
                nc.vector.tensor_tensor_scan(states[:, c, d, :], psum[:, A_BANK + d, :], drive[:, c, d, :], before,
                                             ALU.mult, ALU.add).then_inc(scanned, 1)

            def scans(i, b, next_b, states=state, reused=1):
                scan_channels(i, 0, 0, states, reused)
                drives(i, b, 1)
                scan_channels(i, 0, 1, states, reused)
                scan_channels(i, 1, 0, states, reused)
                if next_b is not None:
                    drives(i + 1, next_b, 0)
                scan_channels(i, 1, 1, states, reused)

            def scan_pair(g, b):
                scans(2 * g, b, b, soft, 2)
                scans(2 * g + 1, b, b, state, 2)

            def gate(b, c):
                t = b * SEQ + c * CH
                for d in range(DT):
                    if b == 0:
                        dve.wait_ge(y_first_ready, DT * c + d + 1)
                        y = y_first[:, c, d, :]
                    else:
                        dve.wait_ge(summed, UNITS * LAST + DT * c + d + 1)
                        y = psum[:, Y_BANK + DT * c + d, :]
                    part = z_gate[:, d, t:t + CH]
                    nc.vector.tensor_tensor(part, part, y, ALU.mult).then_inc(gated, 1)

            drives(0, 0, 0)
            for d in range(DT):
                finish_dt(1, d)
            for i, (q, d) in enumerate(((2, 0), (2, 1), (3, 0), (3, 1))):
                scans(i, 0, 0)
                finish_dt(q, d)
            at = slice((NQ - 1) * CH, NQ * CH)
            dve.wait_ge(dt_ready, DT * NQ)
            nc.vector.tensor_tensor(dtu[:, :, at], dt[:, :, at], u[:, :, at], ALU.mult).then_inc(last_dtu_ready, 1)
            with dve.Fori(2, D_STATE // 2 - 1) as g:
                scan_pair(g, 0)
            scans(D_STATE - 2, 0, 0, soft, 2)
            dve.wait_ge(dtu_ready, DT * (NQ - 1))
            dve.wait_ge(last_dtu_ready, 1)
            scans(D_STATE - 1, 0, 1, state, 2)
            with dve.Fori(D_STATE // 2, D_STATE - 1) as g:
                scan_pair(g, 1)
            scans(LAST - 1, 1, 1, soft, 2)
            for c in range(NCH):
                gate(0, c)
            scans(LAST, 1, None, state, 2)

            def take_moments(rows, g):
                tiles = slice(TPC * g, TPC * (g + 1))
                for j in range(TPC * g, TPC * (g + 1)):
                    nc.vector.bn_stats(stats[:, j, :], rows[:, j, :]).then_inc(dve_step, 1)
                first = step.up(TPC) - TPC
                for j in range(TPC):
                    dve.wait_ge(dve_step, first + j + 1)
                    nc.vector.bn_aggr(moments[:, TPC * g + j, :], stats[:, TPC * g + j, :]).then_inc(dve_step, 1)
                dve.wait_ge(dve_step, step.up(TPC))
                return nc.vector.tensor_scalar(moments[:, tiles, 1], moments[:, tiles, 1], EPS, -0.5, ALU.add, ALU.mult)

            def refine(tiles, ready, value, done):
                dve.wait_ge(ready, value)
                nc.vector.tensor_tensor(newton[:, tiles], rstd[:, tiles], rstd[:, tiles], ALU.mult).then_inc(dve_step, 1)
                dve.wait_ge(dve_step, step.up())
                nc.vector.tensor_tensor(newton[:, tiles], newton[:, tiles], moments[:, tiles, 1], ALU.mult).then_inc(dve_step, 1)
                dve.wait_ge(dve_step, step.up())
                nc.vector.scalar_tensor_tensor(rstd[:, tiles], newton[:, tiles], 1.5, rstd[:, tiles], ALU.add, ALU.mult).then_inc(dve_step, 1)
                dve.wait_ge(dve_step, step.up())
                nc.vector.scalar_tensor_tensor(shift[:, tiles], moments[:, tiles, 0], -1.0, rstd[:, tiles], ALU.mult, ALU.mult).then_inc(done, 1)

            def take_residual(g):
                tiles = slice(TPC * g, TPC * (g + 1))
                bank = [B_BANK, C_BANK, Y_BANK, Y_BANK + 1][g]
                dve.wait_ge(out_projected, g + 1)
                nc.vector.tensor_tensor(x1[:, tiles, :], x_tok[:, tiles, :],
                                        psum[:, bank, :].rearrange("p (j d) -> p j d", d=D_MODEL), ALU.add).then_inc(residual_ready, 1)

            def first_norm_moments(g):
                dve.wait_ge(residual_ready, g + 1)
                take_moments(x1, g).then_inc(moments_ready if g % NCH else dve_step, 1)
                if g % NCH == 0:
                    dve.wait_ge(dve_step, step.up())

            def first_refine(b):
                refine(slice(HALF_TILES * b, HALF_TILES * (b + 1)), rstd_ready, b + 1, shift_ready)

            def chain(ins):
                ins.then_inc(dve_step, 1)
                dve.wait_ge(dve_step, step.up())

            shape = [P, TOP_K, HALF_TILES, N_EXP]

            def choose(b):
                half = slice(HALF_TILES * b, HALF_TILES * (b + 1))
                if b == 0:
                    dve.wait_ge(w_g_summed, 1)
                    nc.vector.tensor_copy(w_g_sum[:, :], psum[:, C_BANK, 0:N_EXP]).then_inc(w_g_sum_copied, 1)
                    dve.wait_ge(w_g_sum_copied, 1)
                chain(nc.vector.tensor_tensor(mean_logits[:, :, :], moments[:, half, 0].unsqueeze(2).to_broadcast(shape[:1] + shape[2:]),
                                              w_g_sum[:, :].unsqueeze(1).to_broadcast(shape[:1] + shape[2:]), ALU.mult))
                dve.wait_ge(logits_ready, b + 1)
                nc.vector.tensor_tensor(logits[:, half, :],
                                        psum[:, B_BANK, HALF_TILES * N_EXP * b:HALF_TILES * N_EXP * (b + 1)].rearrange(
                                            "p (j e) -> p j e", e=N_EXP), mean_logits[:, :, :], ALU.subtract).then_inc(logits_copied, 1)
                dve.wait_ge(logits_copied, b + 1)
                chain(nc.vector.tensor_tensor(logits[:, half, :], logits[:, half, :],
                                              rstd[:, half].unsqueeze(2).to_broadcast(shape[:1] + shape[2:]), ALU.mult))
                for j in range(HALF_TILES * b, HALF_TILES * (b + 1)):
                    nc.vector.max(sorted_logits[:, j, :], logits[:, j, :]).then_inc(dve_step, 1)
                first = step.up(HALF_TILES) - HALF_TILES
                for j in range(HALF_TILES):
                    at = HALF_TILES * b + j
                    dve.wait_ge(dve_step, first + j + 1)
                    nc.vector.max_index(sorted_experts[:, at, :], sorted_logits[:, at, :], logits[:, at, :]).then_inc(dve_step, 1)
                dve.wait_ge(dve_step, step.up(HALF_TILES))
                top = sorted_logits[:, half, 0:TOP_K].rearrange("p j k -> p k j")
                chain(nc.vector.tensor_copy(expert[:, :, half], sorted_experts[:, half, 0:TOP_K].rearrange("p j k -> p k j")))
                dve.wait_ge(consts_made, 1)
                nc.vector.tensor_tensor(chosen[:, b, :, :, :], expert[:, :, half].unsqueeze(3).to_broadcast(shape),
                                        expert_number[:, :].unsqueeze(1).unsqueeze(1).to_broadcast(shape), ALU.is_equal).then_inc(chosen_ready, 1)
                chain(nc.vector.tensor_scalar(peak[:, half], top[:, 0, :], NEG_INF, None, ALU.max))
                nc.vector.tensor_scalar(above[:, TOP_K, half], peak[:, half], -1.0, NEG_INF, ALU.mult, ALU.add).then_inc(above_ready, 1)
                nc.vector.tensor_tensor(above[:, 0:TOP_K, half], top, peak[:, half].unsqueeze(1).to_broadcast([P, TOP_K, HALF_TILES]),
                                        ALU.subtract).then_inc(above_ready, 1)
                for k, offset in enumerate((-1, CAPACITY)):
                    nc.vector.tensor_scalar(slot_base[:, k, half], expert[:, k, half], float(CAPACITY), float(4 * SLOTS + offset),
                                            ALU.mult, ALU.add).then_inc(dve_step, 1)
                    step.up()
                dve.wait_ge(exps_ready, b + 1)
                chain(nc.vector.tensor_tensor(denom[:, half], exps[:, 0, half], exps[:, 1, half], ALU.add))
                chain(nc.vector.scalar_tensor_tensor(denom[:, half], exps[:, TOP_K, half], float(N_EXP - TOP_K), denom[:, half], ALU.mult, ALU.add))
                chain(nc.vector.reciprocal(denom[:, half], denom[:, half]))
                chain(nc.vector.tensor_tensor(weight[:, :, half], exps[:, 0:TOP_K, half],
                                              denom[:, half].unsqueeze(1).to_broadcast([P, TOP_K, HALF_TILES]), ALU.mult))

            def place(b):
                half = slice(HALF_TILES * b, HALF_TILES * (b + 1))
                dve.wait_ge(ranks_counted, b + 1)
                at = slice(b * COUNTS, (b + 1) * COUNTS)
                chain(nc.vector.tensor_copy(run_totals[:, :, :, HALF_TILES * b + 1:HALF_TILES * (b + 1) + 1],
                                            psum[:, C_BANK, (BATCH + b) * COUNTS:(BATCH + b + 1) * COUNTS].rearrange(
                                                "p (k j e) -> p e k j", k=TOP_K, e=N_EXP)))
                flat = lambda a: a[:, :, :, :].rearrange("p a b c -> p (a b c)")
                chain(nc.vector.tensor_tensor_scan(flat(run_before), flat(run_keep), flat(run_totals), 0.0, ALU.mult, ALU.add))
                nc.vector.tensor_tensor(ranks[:, :, :, :], run_before[:, :, :, half].rearrange("p e k j -> p k j e"),
                                        psum[:, C_BANK, at].rearrange("p (k j e) -> p k j e", k=TOP_K, e=N_EXP), ALU.add).then_inc(ranks_taken, 1)
                dve.wait_ge(ranks_taken, b + 1)
                nc.vector.tensor_tensor(firsts[:, :, :], chosen[:, b, 1, :, :],
                                        run_before[:, :, 0, TILES].unsqueeze(1).to_broadcast(shape[:1] + shape[2:]), ALU.mult).then_inc(dve_step, 1)
                step.up()
                chain(nc.vector.tensor_tensor(ranks[:, :, :, :], ranks[:, :, :, :], chosen[:, b, :, :, :], ALU.mult))
                nc.vector.tensor_reduce(first_count[:, :], firsts[:, :, :], axis=AX.X, op=ALU.add).then_inc(dve_step, 1)
                step.up()
                chain(nc.vector.tensor_reduce(rank[:, :, half], ranks[:, :, :, :], axis=AX.X, op=ALU.add))
                nc.vector.tensor_tensor(first_count[:, :], first_count[:, :], rank[:, 1, half], ALU.add).then_inc(dve_step, 1)
                step.up()
                nc.vector.tensor_tensor(slot_base[:, 0, half], slot_base[:, 0, half], rank[:, 0, half], ALU.add).then_inc(dve_step, 1)
                step.up()
                chain(nc.vector.tensor_tensor(slot_base[:, 1, half], slot_base[:, 1, half], rank[:, 1, half], ALU.subtract))
                nc.vector.tensor_scalar(kept[:, 0, half], rank[:, 0, half], float(CAPACITY), None, ALU.is_le).then_inc(dve_step, 1)
                step.up()
                chain(nc.vector.tensor_scalar(kept[:, 1, half], first_count[:, :], float(CAPACITY), None, ALU.is_le))
                nc.vector.tensor_tensor(sent[:, :, half, ROW_WEIGHT], weight[:, :, half], kept[:, :, half], ALU.mult).then_inc(slots_ready, 1)
                nc.vector.scalar_tensor_tensor(scatter_at[:, :, half], kept[:, :, half], -float(4 * SLOTS), slot_base[:, :, half],
                                               ALU.mult, ALU.add).then_inc(slots_ready, 1)

            take_residual(0)
            first_norm_moments(0)
            take_residual(1)
            first_norm_moments(1)
            gate(1, 0)
            first_refine(0)
            choose(0)
            place(0)
            gate(1, 1)
            take_residual(2)
            take_residual(3)
            first_norm_moments(2)
            first_norm_moments(3)
            first_refine(1)
            choose(1)
            place(1)

            def copy_turned(g, i):
                e = 2 * g + i
                dve.wait_ge(rows_turned, e + 1)
                nc.vector.tensor_scalar(tags[:, bass.ds(e, 1), :, :].rearrange("p a s k -> p (a s) k"),
                                        rows_in[:, i, :, ROW_TO:ROW], 1.0, None, ALU.mult).then_inc(tags_copied, 1)
                if not (isinstance(g, int) and g == 0):
                    dve.wait_ge(fc_done, HT * (e - 1))
                nc.vector.tensor_copy(rows_chan[:, i, :], psum[:, 0:2, :].rearrange("p b c -> p (b c)")[:, 0:CAPACITY]).then_inc(rows_chan_ready, 1)

            def copy_results(g, i):
                e = 2 * g + i
                if not (isinstance(g, int) and g == 0):
                    dve.wait_ge(results_sent[i], 16 * SLOT_TILES * g)
                dve.wait_ge(tags_copied, e + 1)
                tag = tags[:, bass.ds(e, 1), :, :].rearrange("p a s k -> p (a s) k")
                nc.vector.tensor_scalar(result_at[:, i, :], tag[:, :, 0], 1.0, None, ALU.mult).then_inc(result_tagged, 1)
                nc.vector.tensor_scalar(result_weight[:, i, :], tag[:, :, 1], 1.0, None, ALU.mult).then_inc(result_tagged, 1)
                dve.wait_ge(result_tagged, 2 * (e + 1))
                if isinstance(g, int) and g == PAIRS - 1:
                    for s in range(SLOT_TILES):
                        dve.wait_ge(last_proj_done, SLOT_TILES * i + s + 1)
                        nc.vector.tensor_scalar(rows_out[:, i, s, :], psum[:, LAST_BANKS[i][s], 0:P],
                                                result_weight[:, i, s:s + 1], None, ALU.mult).then_inc(last_rows_out_ready, 1)
                    return
                dve.wait_ge(proj_done, e + 1)
                nc.vector.tensor_tensor(rows_out[:, i, :, :],
                                        psum[:, 6:8, :].rearrange("p b (j d) -> p (b j) d", d=D_MODEL)[:, 0:SLOT_TILES, :],
                                        result_weight[:, i, :].unsqueeze(2).to_broadcast([P, SLOT_TILES, D_MODEL]),
                                        ALU.mult).then_inc(rows_out_ready, 1)

            for i in range(2):
                copy_turned(0, i)
            for i in range(2):
                copy_turned(1, i)
                copy_results(0, i)
            with dve.Fori(2, PAIRS) as g:
                for i in range(2):
                    copy_turned(g, i)
                    copy_results(g - 1, i)
            for i in range(2):
                copy_results(PAIRS - 1, i)

            for g in range(GROUPS):
                tiles = slice(TPC * g, TPC * (g + 1))
                dve.wait_ge(results_loaded[1][g], 16)
                dve.wait_ge(first_added, g + 1)
                chain(nc.vector.tensor_tensor(final[:, tiles, :], final[:, tiles, :],
                                              results[:, TILES + TPC * g:TILES + TPC * (g + 1), :], ALU.add))
                take_moments(final, g).then_inc(moments2_ready, 1)
                if g:
                    refine(slice(TPC * (g - 1), TPC * g), rstd2_ready, g, shift2_ready)
            refine(slice(TPC * (GROUPS - 1), TILES), rstd2_ready, GROUPS, shift2_ready)
            for g in range(NCH, GROUPS):
                dve.wait_ge(shift2_ready, g + 1)
                for j in range(TPC * g + TPC // 2, TPC * (g + 1)):
                    nc.vector.tensor_scalar(final[:, j, :], final[:, j, :], rstd[:, j:j + 1], shift[:, j:j + 1],
                                            ALU.mult, ALU.add).then_inc(late_out_ready, 1)


def kernel(L0_attn_x, L0_attn_W_in, L0_attn_conv_w, L0_attn_conv_b, L0_attn_W_x, L0_attn_W_dt, L0_attn_b_dt,
           L0_attn_A_log, L0_attn_D, L0_attn_W_out, L0_ffn_w_g, L0_ffn_c_fc, L0_ffn_c_proj):
    import concourse.bacc as bacc
    from concourse.bass_utils import run_bass_kernel_spmd

    columns = [np.asarray(a).reshape(D_INNER, -1) for a in (L0_attn_conv_w, L0_attn_conv_b, L0_attn_b_dt, L0_attn_D)]
    channel_values = np.concatenate(columns, axis=1).reshape(DT, P, D_CONV + 3).transpose(1, 0, 2)
    inputs = {"x": L0_attn_x, "W_in": L0_attn_W_in, "channel_values": channel_values, "W_x": L0_attn_W_x, "W_dt": L0_attn_W_dt,
              "A_log": L0_attn_A_log, "W_out": L0_attn_W_out, "w_g": L0_ffn_w_g, "c_fc": L0_ffn_c_fc, "c_proj": L0_ffn_c_proj}
    arrays = {f"in_{name}": np.ascontiguousarray(a) for name, a in inputs.items()}

    nc = bacc.Bacc("TRN2", target_bir_lowering=False, num_devices=1)
    args = [nc.dram_tensor(name, a.shape, mybir.dt.from_np(a.dtype), kind="ExternalInput").ap() for name, a in arrays.items()]
    args.append(nc.dram_tensor("out", (BATCH, SEQ, D_MODEL), F32, kind="ExternalOutput").ap())
    layer_program(nc, *args)
    result = run_bass_kernel_spmd(nc, [arrays], core_ids=[0])
    return result.results[0]["out"]
```
